# Optimizing a Trainium2 kernel written in Bass

```python
import numpy as np
import jax
import jax.numpy as jnp

def _softmax(x, axis=-1):
    return jax.nn.softmax(x, axis=axis)

def _gelu(x):
    return jax.nn.gelu(x, approximate=True)

def _silu(x):
    return jax.nn.silu(x)

def _sigmoid(x):
    return jax.nn.sigmoid(x)

def _layernorm(x, axis=-1, eps=1e-05):
    m = jnp.mean(x, axis=axis, keepdims=True)
    v = jnp.var(x, axis=axis, keepdims=True)
    return (x - m) / jnp.sqrt(v + eps)

def _scatter_add(tgt, idx, src, axis=0):
    return tgt.at[idx].add(src)

def _segment_sum(src, seg, n):
    return jax.ops.segment_sum(src, seg, n)
kernel_name = 'mk_xattn_ffn_d2_seqx_r4_399442'

def setup_inputs(seed: int=0):
    np.random.seed(seed)
    _w = jnp.asarray

    def _rec_inputs():
        import jax
        import jax.numpy as jnp
        _rk = jax.random.key(seed)
        x = -0.0002928 + 1 * jax.random.normal(jax.random.fold_in(_rk, 1), (4, 512, 256), jnp.float32)
        _lenS = 512 - jax.random.randint(jax.random.fold_in(_rk, 7), (4,), 0, max(1, 512 // 4) + 1, jnp.int32)
        _lenS2 = 512 - jax.random.randint(jax.random.fold_in(_rk, 8), (4,), 0, max(1, 512 // 4) + 1, jnp.int32)
        _ctx_1024P = jax.random.normal(jax.random.fold_in(_rk, 11), (4, 16, 256), jnp.float32)
        _ctx_1024c = jax.random.dirichlet(jax.random.fold_in(_rk, 511), 0.3 * jnp.ones((16,), jnp.float32), (4, 512))
        _ctx_1024t = jnp.einsum('bsk,bkd->bsd', _ctx_1024c, _ctx_1024P)
        _ctx_1024t = _ctx_1024t * jax.lax.rsqrt(jnp.mean(jnp.square(_ctx_1024t)) + 1e-12) * 0.953939
        ctx_1024 = -1.39393e-06 + 0.999914 * (_ctx_1024t + 0.3 * jax.random.normal(jax.random.fold_in(_rk, 611), (4, 512, 256), jnp.float32))
        _validS = jnp.arange(512)[None, :] < _lenS[:, None]
        _validS2 = jnp.arange(512)[None, :] < _lenS2[:, None]
        _causal = jnp.tril(jnp.ones((512, 512), dtype=bool))
        mask_Bx1xSxS2_ik1 = jnp.where(jnp.broadcast_to(_validS2[:, None, None, :], (4, 1, 512, 512)), 1, 0).astype(jnp.int32)
        return (x, ctx_1024, mask_Bx1xSxS2_ik1)
    x, ctx_1024, mask_Bx1xSxS2_ik1 = _rec_inputs()

    def _L0_xattn_setup():
        import jax, jax.numpy as jnp
        import numpy as np
        HEADS = 16
        D_K = 64
        D_V = 64
        D_MODEL = 256
        N, T = (2, 512)
        key = jax.random.key(seed)
        ks = jax.random.split(key, 9)
        s = 1.0 / np.sqrt(D_MODEL)
        return {'queries': jax.random.normal(ks[0], (N, T, D_MODEL), dtype=jnp.float32), 'keys': jax.random.normal(ks[1], (N, T, D_MODEL), dtype=jnp.float32), 'values': jax.random.normal(ks[2], (N, T, D_MODEL), dtype=jnp.float32), 'mask': jax.random.randint(ks[3], (N, 1, T, T), 0, 2, dtype=jnp.int32), 'Wq': jax.random.normal(ks[4], (D_MODEL, HEADS * D_K), dtype=jnp.float32) * s, 'Wk': jax.random.normal(ks[5], (D_MODEL, HEADS * D_K), dtype=jnp.float32) * s, 'Wv': jax.random.normal(ks[6], (D_MODEL, HEADS * D_V), dtype=jnp.float32) * s, 'Wo': jax.random.normal(ks[7], (HEADS * D_V, D_MODEL), dtype=jnp.float32) * s}
    _L0_xattn_all = _L0_xattn_setup()
    _L0_xattn_in = {k: v for k, v in _L0_xattn_all.items() if k in ('Wq', 'Wk', 'Wv', 'Wo')}
    del _L0_xattn_all

    def _L0_ffn_setup():
        import jax, jax.numpy as jnp
        import numpy as np
        EMBED_DIM = 256
        MLP_RATIO = 4
        NUM_EXPERTS = 8
        CAPACITY = 1.0
        LN_EPS = 1e-05

        def _layernorm(y, gamma, beta):
            mu = jnp.mean(y, axis=-1, keepdims=True)
            var = jnp.mean(jnp.square(y - mu), axis=-1, keepdims=True)
            return (y - mu) * jax.lax.rsqrt(var + LN_EPS) * gamma + beta
        key = jax.random.key(seed)
        k0, k1, k2, k3, k4, k5 = jax.random.split(key, 6)
        d = EMBED_DIM
        dd = EMBED_DIM * MLP_RATIO
        n = NUM_EXPERTS
        x = jax.random.normal(k0, (4, 512, d), dtype=jnp.float32)
        gate_w = jax.random.normal(k1, (n, d), dtype=jnp.float32) * 0.02
        ln_gamma = jnp.ones((d,), dtype=jnp.float32)
        ln_beta = jnp.zeros((d,), dtype=jnp.float32)
        fc1s = jax.random.normal(k2, (n, dd, d), dtype=jnp.float32) * (1.0 / np.sqrt(d))
        b1s = jax.random.normal(k3, (n, dd), dtype=jnp.float32) * 0.02
        fc2s = jax.random.normal(k4, (n, d, dd), dtype=jnp.float32) * (1.0 / np.sqrt(dd))
        b2s = jax.random.normal(k5, (n, d), dtype=jnp.float32) * 0.02
        return {'x': x, 'gate_w': gate_w, 'ln_gamma': ln_gamma, 'ln_beta': ln_beta, 'fc1s': fc1s, 'b1s': b1s, 'fc2s': fc2s, 'b2s': b2s}
    _L0_ffn_all = _L0_ffn_setup()
    _L0_ffn_in = {k: v for k, v in _L0_ffn_all.items() if k in ('gate_w', 'ln_gamma', 'ln_beta', 'fc1s', 'b1s', 'fc2s', 'b2s')}
    del _L0_ffn_all

    def _L1_xattn_setup():
        import jax, jax.numpy as jnp
        import numpy as np
        D_MODEL = 256
        N_HEADS = 16
        D_HEAD = D_MODEL // N_HEADS
        WINDOW = 128

        def _attn(q, k, v, Wq, bq, Wk, bk, Wv, bv, Wo, bo):
            B, L, D = q.shape
            H, Dh = (N_HEADS, D_HEAD)
            qh = (q @ Wq.T + bq).reshape(B, L, H, Dh).transpose(0, 2, 1, 3)
            kh = (k @ Wk.T + bk).reshape(B, L, H, Dh).transpose(0, 2, 1, 3)
            vh = (v @ Wv.T + bv).reshape(B, L, H, Dh).transpose(0, 2, 1, 3)
            scale = jnp.sqrt(jnp.asarray(Dh, q.dtype))
            scores = jnp.einsum('bhqd,bhkd->bhqk', qh, kh) / scale
            pos = jnp.arange(L)
            band = jnp.abs(pos[:, None] - pos[None, :]) <= WINDOW
            scores = jnp.where(band[None, None], scores, -jnp.inf)
            w = jax.nn.softmax(scores, axis=-1)
            out = jnp.einsum('bhqk,bhkd->bhqd', w, vh)
            out = out.transpose(0, 2, 1, 3).reshape(B, L, D)
            return out @ Wo.T + bo
        key = jax.random.key(seed)
        ks = jax.random.split(key, 11)
        B, L = (2, 512)
        s = 1.0 / np.sqrt(D_MODEL)
        inp = {'q': jax.random.normal(ks[0], (B, L, D_MODEL), jnp.float32), 'k': jax.random.normal(ks[1], (B, L, D_MODEL), jnp.float32), 'v': jax.random.normal(ks[2], (B, L, D_MODEL), jnp.float32), 'Wq': jax.random.normal(ks[3], (D_MODEL, D_MODEL), jnp.float32) * s, 'bq': jnp.zeros((D_MODEL,), jnp.float32), 'Wk': jax.random.normal(ks[4], (D_MODEL, D_MODEL), jnp.float32) * s, 'bk': jnp.zeros((D_MODEL,), jnp.float32), 'Wv': jax.random.normal(ks[5], (D_MODEL, D_MODEL), jnp.float32) * s, 'bv': jnp.zeros((D_MODEL,), jnp.float32), 'Wo': jax.random.normal(ks[6], (D_MODEL, D_MODEL), jnp.float32) * s, 'bo': jnp.zeros((D_MODEL,), jnp.float32)}
        return inp
    _L1_xattn_all = _L1_xattn_setup()
    _L1_xattn_in = {k: v for k, v in _L1_xattn_all.items() if k in ('Wq', 'bq', 'Wk', 'bk', 'Wv', 'bv', 'Wo', 'bo')}
    del _L1_xattn_all

    def _L1_ffn_setup():
        import jax, jax.numpy as jnp
        import numpy as np
        D_MODEL = 256
        FFN_DIM = 512
        NUM_EXPERTS = 8
        NUM_GROUPS = 4
        EXPERTS_PER_GROUP = NUM_EXPERTS // NUM_GROUPS
        TOP_K = 2
        GROUPS_TOP_K = 1
        EPS = 1e-09

        def _topk_normalized(scores, k):
            vals, idx = jax.lax.top_k(scores, k)
            vals = vals / (jnp.sum(vals, axis=-1, keepdims=True) + EPS)
            return (vals, idx)
        key = jax.random.key(seed)
        ks = jax.random.split(key, 6)
        B, S = (2, 256)
        x = jax.random.normal(ks[0], (B, S, D_MODEL), dtype=jnp.float32)
        sd = 0.02
        macro_w = jax.random.normal(ks[1], (D_MODEL, NUM_GROUPS), dtype=jnp.float32) * sd
        micro_w = jax.random.normal(ks[2], (NUM_GROUPS, D_MODEL, EXPERTS_PER_GROUP), dtype=jnp.float32) * sd
        gate_w = jax.random.normal(ks[3], (NUM_EXPERTS, D_MODEL, FFN_DIM), dtype=jnp.float32) * sd
        up_w = jax.random.normal(ks[4], (NUM_EXPERTS, D_MODEL, FFN_DIM), dtype=jnp.float32) * sd
        down_w = jax.random.normal(ks[5], (NUM_EXPERTS, FFN_DIM, D_MODEL), dtype=jnp.float32) * sd
        return {'x': x, 'macro_w': macro_w, 'micro_w': micro_w, 'gate_w': gate_w, 'up_w': up_w, 'down_w': down_w}
    _L1_ffn_all = _L1_ffn_setup()
    _L1_ffn_in = {k: v for k, v in _L1_ffn_all.items() if k in ('macro_w', 'micro_w', 'gate_w', 'up_w', 'down_w')}
    del _L1_ffn_all
    return {'x': x, 'ctx_1024': ctx_1024, 'mask_Bx1xSxS2_ik1': mask_Bx1xSxS2_ik1, 'L0_xattn_Wq': _L0_xattn_in['Wq'], 'L0_xattn_Wk': _L0_xattn_in['Wk'], 'L0_xattn_Wv': _L0_xattn_in['Wv'], 'L0_xattn_Wo': _L0_xattn_in['Wo'], 'L0_ffn_gate_w': _L0_ffn_in['gate_w'], 'L0_ffn_ln_gamma': _L0_ffn_in['ln_gamma'], 'L0_ffn_ln_beta': _L0_ffn_in['ln_beta'], 'L0_ffn_fc1s': _L0_ffn_in['fc1s'], 'L0_ffn_b1s': _L0_ffn_in['b1s'], 'L0_ffn_fc2s': _L0_ffn_in['fc2s'], 'L0_ffn_b2s': _L0_ffn_in['b2s'], 'L1_xattn_Wq': _L1_xattn_in['Wq'], 'L1_xattn_bq': _L1_xattn_in['bq'], 'L1_xattn_Wk': _L1_xattn_in['Wk'], 'L1_xattn_bk': _L1_xattn_in['bk'], 'L1_xattn_Wv': _L1_xattn_in['Wv'], 'L1_xattn_bv': _L1_xattn_in['bv'], 'L1_xattn_Wo': _L1_xattn_in['Wo'], 'L1_xattn_bo': _L1_xattn_in['bo'], 'L1_ffn_macro_w': _L1_ffn_in['macro_w'], 'L1_ffn_micro_w': _L1_ffn_in['micro_w'], 'L1_ffn_gate_w': _L1_ffn_in['gate_w'], 'L1_ffn_up_w': _L1_ffn_in['up_w'], 'L1_ffn_down_w': _L1_ffn_in['down_w']}

def reference(x, ctx_1024, mask_Bx1xSxS2_ik1, L0_xattn_Wq, L0_xattn_Wk, L0_xattn_Wv, L0_xattn_Wo, L0_ffn_gate_w, L0_ffn_ln_gamma, L0_ffn_ln_beta, L0_ffn_fc1s, L0_ffn_b1s, L0_ffn_fc2s, L0_ffn_b2s, L1_xattn_Wq, L1_xattn_bq, L1_xattn_Wk, L1_xattn_bk, L1_xattn_Wv, L1_xattn_bv, L1_xattn_Wo, L1_xattn_bo, L1_ffn_macro_w, L1_ffn_micro_w, L1_ffn_gate_w, L1_ffn_up_w, L1_ffn_down_w):
    import jax
    import jax.numpy as jnp

    def _L0_xattn_ref(queries, keys, values, mask, Wq, Wk, Wv, Wo):
        import jax, jax.numpy as jnp
        import numpy as np
        HEADS = 16
        D_K = 64
        D_V = 64
        D_MODEL = 256
        N, T = (2, 512)
        n, t, _ = queries.shape
        Qh = (queries @ Wq).reshape(n, t, HEADS, D_K)
        Kh = (keys @ Wk).reshape(n, t, HEADS, D_K)
        Vh = (values @ Wv).reshape(n, t, HEADS, D_V)
        scale = 1.0 / jnp.sqrt(jnp.asarray(D_K, dtype=queries.dtype))
        energy = jnp.einsum('nqhd,nkhd->nhqk', Qh, Kh) * scale
        energy = jnp.where(mask == 0, jnp.asarray(-1e+20, dtype=energy.dtype), energy)
        attention = jax.nn.softmax(energy, axis=-1)
        heads_out = jnp.einsum('nhqk,nkhd->nqhd', attention, Vh)
        concat = heads_out.reshape(n, t, HEADS * D_V)
        return concat @ Wo

    def _L0_ffn_ref(x, gate_w, ln_gamma, ln_beta, fc1s, b1s, fc2s, b2s):
        import jax, jax.numpy as jnp
        import numpy as np
        EMBED_DIM = 256
        MLP_RATIO = 4
        NUM_EXPERTS = 8
        CAPACITY = 1.0
        LN_EPS = 1e-05

        def _layernorm(y, gamma, beta):
            mu = jnp.mean(y, axis=-1, keepdims=True)
            var = jnp.mean(jnp.square(y - mu), axis=-1, keepdims=True)
            return (y - mu) * jax.lax.rsqrt(var + LN_EPS) * gamma + beta
        og_shape = x.shape
        d = og_shape[-1]
        xf = x.reshape(-1, d)
        bs = xf.shape[0]
        n = gate_w.shape[0]
        k = int(bs * CAPACITY) // n
        scores = xf @ gate_w.T
        scores = (jnp.tanh(scores) + 1.0) * 0.5
        vals, idx = jax.lax.top_k(scores.T, k)
        kept_w = vals.T
        flat_idx = idx.T.reshape(-1)
        y = xf[flat_idx].reshape(k, n, d)
        y = _layernorm(y, ln_gamma, ln_beta)
        h = jnp.einsum('knd,nfd->knf', y, fc1s) + b1s
        h = jax.nn.gelu(h, approximate=True)
        o = jnp.einsum('knf,ndf->knd', h, fc2s) + b2s
        o = o * kept_w[:, :, None]
        out = xf.at[flat_idx].add(o.reshape(k * n, d))
        return out.reshape(og_shape)

    def _L1_xattn_ref(q, k, v, Wq, bq, Wk, bk, Wv, bv, Wo, bo):
        import jax, jax.numpy as jnp
        import numpy as np
        D_MODEL = 256
        N_HEADS = 16
        D_HEAD = D_MODEL // N_HEADS
        WINDOW = 128

        def _attn(q, k, v, Wq, bq, Wk, bk, Wv, bv, Wo, bo):
            B, L, D = q.shape
            H, Dh = (N_HEADS, D_HEAD)
            qh = (q @ Wq.T + bq).reshape(B, L, H, Dh).transpose(0, 2, 1, 3)
            kh = (k @ Wk.T + bk).reshape(B, L, H, Dh).transpose(0, 2, 1, 3)
            vh = (v @ Wv.T + bv).reshape(B, L, H, Dh).transpose(0, 2, 1, 3)
            scale = jnp.sqrt(jnp.asarray(Dh, q.dtype))
            scores = jnp.einsum('bhqd,bhkd->bhqk', qh, kh) / scale
            pos = jnp.arange(L)
            band = jnp.abs(pos[:, None] - pos[None, :]) <= WINDOW
            scores = jnp.where(band[None, None], scores, -jnp.inf)
            w = jax.nn.softmax(scores, axis=-1)
            out = jnp.einsum('bhqk,bhkd->bhqd', w, vh)
            out = out.transpose(0, 2, 1, 3).reshape(B, L, D)
            return out @ Wo.T + bo
        return _attn(q, k, v, Wq, bq, Wk, bk, Wv, bv, Wo, bo)

    def _L1_ffn_ref(x, macro_w, micro_w, gate_w, up_w, down_w):
        import jax, jax.numpy as jnp
        import numpy as np
        D_MODEL = 256
        FFN_DIM = 512
        NUM_EXPERTS = 8
        NUM_GROUPS = 4
        EXPERTS_PER_GROUP = NUM_EXPERTS // NUM_GROUPS
        TOP_K = 2
        GROUPS_TOP_K = 1
        EPS = 1e-09

        def _topk_normalized(scores, k):
            vals, idx = jax.lax.top_k(scores, k)
            vals = vals / (jnp.sum(vals, axis=-1, keepdims=True) + EPS)
            return (vals, idx)
        B, S, D = x.shape
        T = B * S
        xf = x.reshape(T, D)
        macro_scores = jax.nn.sigmoid(xf @ macro_w)
        mv, mi = _topk_normalized(macro_scores, GROUPS_TOP_K)
        macro_full = jnp.sum(jax.nn.one_hot(mi, NUM_GROUPS, dtype=xf.dtype) * mv[..., None], axis=1)
        micro_scores = jax.nn.sigmoid(jnp.einsum('td,gde->tge', xf, micro_w))
        uv, ui = _topk_normalized(micro_scores, TOP_K)
        micro_full = jnp.sum(jax.nn.one_hot(ui, EXPERTS_PER_GROUP, dtype=xf.dtype) * uv[..., None], axis=2)
        w = (macro_full[:, :, None] * micro_full).reshape(T, NUM_EXPERTS)
        gate = jax.nn.silu(jnp.einsum('td,edf->tef', xf, gate_w))
        up = jnp.einsum('td,edf->tef', xf, up_w)
        h = gate * up
        out = jnp.einsum('te,tef,efd->td', w, h, down_w)
        return out.reshape(B, S, D)
    x = x + _L0_xattn_ref(_layernorm(x, axis=-1), ctx_1024, ctx_1024, mask_Bx1xSxS2_ik1, L0_xattn_Wq, L0_xattn_Wk, L0_xattn_Wv, L0_xattn_Wo)
    x = x + _L0_ffn_ref(_layernorm(x, axis=-1), L0_ffn_gate_w, L0_ffn_ln_gamma, L0_ffn_ln_beta, L0_ffn_fc1s, L0_ffn_b1s, L0_ffn_fc2s, L0_ffn_b2s)
    x = x + _L1_xattn_ref(_layernorm(x, axis=-1), ctx_1024, ctx_1024, L1_xattn_Wq, L1_xattn_bq, L1_xattn_Wk, L1_xattn_bk, L1_xattn_Wv, L1_xattn_bv, L1_xattn_Wo, L1_xattn_bo)
    x = x + _L1_ffn_ref(_layernorm(x, axis=-1), L1_ffn_macro_w, L1_ffn_micro_w, L1_ffn_gate_w, L1_ffn_up_w, L1_ffn_down_w)
    return x

_drawn_inputs = setup_inputs


def setup_inputs(seed=0):
    import zlib

    import numpy as np

    out = dict(_drawn_inputs(seed))
    spreads = {'L0_ffn_ln_gamma': (1.0, 0.2),
     'L0_ffn_ln_beta': (0.0, 0.43),
     'L1_xattn_bq': (0.0, 0.8),
     'L1_xattn_bk': (0.0, 0.8),
     'L1_xattn_bv': (0.0, 0.1),
     'L1_xattn_bo': (0.0, 0.1)}
    factors = {'L0_ffn_b1s': 8.0,
     'L0_ffn_b2s': 8.0,
     'L1_ffn_macro_w': 8.0,
     'L1_ffn_micro_w': 8.0,
     'L1_ffn_gate_w': 8.0,
     'L1_ffn_up_w': 8.0,
     'L1_ffn_down_w': 8.0}
    for name, (base, spread) in spreads.items():
        noise = np.random.default_rng([zlib.crc32(name.encode()), seed]).standard_normal(out[name].shape)
        drawn = base * np.exp(spread * noise) if base else spread * noise
        out[name] = jnp.asarray(drawn.astype(out[name].dtype))
    for name, factor in factors.items():
        out[name] = (out[name] * factor).astype(out[name].dtype)
    return out
```

```python
from contextlib import ExitStack

import numpy as np

import concourse.bass as bass
from concourse import mybir

ALU = mybir.AluOpType
ACT = mybir.ActivationFunctionType
AX = mybir.AxisListType
F32 = mybir.dt.float32
F16 = mybir.dt.float16
BF16 = mybir.dt.bfloat16
I32 = mybir.dt.int32

P = 128
B, S, D = 4, 512, 256
NT = B * S // P
QT = S // P
DT = D // P
HEADS = 16
DK = 64
CW = HEADS * DK
CT = CW // P
PAIRS = HEADS // 2
UNITS = 2 * QT
EPS = 1e-5
SCALE0 = DK ** -0.5
MASKED = -1e20 / SCALE0


def make_tensors(nc, ctx):
    def sb(name, shape, dt=F32):
        return ctx.enter_context(nc.sbuf_tensor(name, shape, dt))

    def ps(name, shape, dt=F32):
        return ctx.enter_context(nc.psum_tensor(name, shape, dt))

    return sb, ps


class Split:

    def __init__(self, sb, name, shape):
        self.hi = sb(name + "_hi", shape, F16)
        self.lo = sb(name + "_lo", shape, F16)


def layernorm_stats(nc, dve, T, call, src, stats, mv, sd):
    for t in range(NT):
        nc.vector.bn_stats(stats[:, t, :], src[:, t, :]).then_inc(T.stat_done, 1)
    dve.wait_ge(T.stat_done, (call + 1) * NT)
    for t in range(NT):
        nc.vector.bn_aggr(mv[:, t, :], stats[:, t, :]).then_inc(T.mv_done, 1)
    dve.wait_ge(T.mv_done, (call + 1) * NT)
    nc.vector.tensor_scalar(sd[:], mv[:, :, 1], EPS, None, ALU.add).then_inc(T.var_eps, 1)
    dve.wait_ge(T.sd_done, call + 1)


def layernorm_root(nc, act, T, call, sd):
    act.wait_ge(T.var_eps, call + 1)
    nc.scalar.activation(sd[:], sd[:], ACT.Sqrt).then_inc(T.sd_done, 1)


def phase_prepare(nc, sem, sb_x, T, dram):
    with ExitStack() as ctx:
        sb, ps = make_tensors(nc, ctx)
        ctx_raw = sb("ctx_raw", [P, DT, B * S])
        w_raw = [sb(f"w_raw{i}", [P, 2048]) for i in range(4)]
        stats = sb("stats", [P, NT, 6])
        mv = sb("mv", [P, NT, 2])
        sd = sb("sd", [P, NT])
        rstd = sb("rstd", [P, NT])
        z = [sb(f"z{i}", [P, D]) for i in range(4)]
        bank = [ps(f"zt_bank{i}", [P, DT, 2 * P]) for i in range(2)]
        x_in, ctx_in, w_in = sem("x_in"), sem("ctx_in"), sem("w_in")
        ident_set, ident_ok = sem("ident_set"), sem("ident_ok")
        w_hi, ctx_hi = sem("w_hi"), sem("ctx_hi")
        rstd_done = sem("rstd_done")
        z_done, zt_done, zt_hi, zt_lo = sem("z_done"), sem("zt_done"), sem("zt_hi"), sem("zt_lo")
        weights = [T.wq0, T.wk0, T.wv0, T.wo0]
        with nc.Block() as block:

            @block.sync
            def _(sp):
                sp.dma_start(T.x[:], dram["x"].rearrange("(t p) d -> p t d", p=P)).then_inc(x_in, 16)
                sp.dma_start(ctx_raw[:], dram["ctx_t"].rearrange("(c p) t -> p c t", p=P)).then_inc(ctx_in, 16)
                for i, name in enumerate(("wq0", "wk0", "wv0", "wo0")):
                    sp.dma_start(w_raw[i][:].rearrange("p (c n) -> p c n", n=dram[name].shape[1]),
                                 dram[name].rearrange("(c p) n -> p c n", p=P)).then_inc(w_in, 16)

            @block.gpsimd
            def _(pool):
                pool.memset(T.ident[:], 0.0).then_inc(ident_set, 1)
                pool.wait_ge(ident_set, 1)
                pool.affine_select(out=T.ident[:], in_=T.ident[:], compare_op=ALU.not_equal, fill=1.0, base=0,
                                   pattern=[[-1, P]], channel_multiplier=1).then_inc(ident_ok, 1)
                pool.wait_ge(ctx_hi, 1)
                pool.tensor_tensor(T.ctx_t.lo[:], ctx_raw[:], T.ctx_t.hi[:], ALU.subtract)
                pool.wait_ge(w_hi, 4)
                pool.tensor_tensor(weights[3].lo[:].rearrange("p c n -> p (c n)"), w_raw[3][:],
                                   weights[3].hi[:].rearrange("p c n -> p (c n)"), ALU.subtract)

            @block.scalar
            def _(act):
                layernorm_root(nc, act, T, 0, sd)
                act.wait_ge(ctx_in, 16)
                nc.scalar.activation(T.ctx_t.hi[:], ctx_raw[:], ACT.Copy).then_inc(ctx_hi, 1)
                act.wait_ge(w_in, 64)
                for i, w in enumerate(weights):
                    nc.scalar.activation(w.hi[:].rearrange("p c n -> p (c n)"), w_raw[i][:], ACT.Copy).then_inc(w_hi, 1)
                for g in range(NT // 2):
                    act.wait_ge(zt_done, g + 1)
                    nc.scalar.activation(T.z_t.hi[:, :, g * 2 * P:(g + 1) * 2 * P], bank[g % 2][:], ACT.Copy).then_inc(zt_hi, 1)

            @block.vector
            def _(dve):
                dve.wait_ge(x_in, 16)
                layernorm_stats(nc, dve, T, 0, T.x, stats, mv, sd)
                nc.vector.reciprocal(rstd[:], sd[:]).then_inc(rstd_done, 1)
                dve.wait_ge(rstd_done, 1)

                def zt_lo_part(g):
                    dve.wait_ge(zt_hi, g + 1)
                    cols = slice(g * 2 * P, (g + 1) * 2 * P)
                    nc.vector.tensor_tensor(T.z_t.lo[:, :, cols], bank[g % 2][:], T.z_t.hi[:, :, cols], ALU.subtract).then_inc(zt_lo, 1)

                for t in range(NT):
                    if t >= 4:
                        dve.wait_ge(zt_done, (t - 4) // 2 + 1)
                    nc.vector.tensor_scalar(z[t % 4][:], T.x[:, t, :], mv[:, t, 0:1], rstd[:, t:t + 1],
                                            ALU.subtract, ALU.mult).then_inc(z_done, 1)
                    if t % 2 == 1 and t >= 3:
                        zt_lo_part(t // 2 - 1)
                zt_lo_part(NT // 2 - 1)
                for i in range(3):
                    dve.wait_ge(w_hi, i + 1)
                    nc.vector.tensor_tensor(weights[i].lo[:].rearrange("p c n -> p (c n)"), w_raw[i][:],
                                            weights[i].hi[:].rearrange("p c n -> p (c n)"), ALU.subtract)

            @block.tensor
            def _(pe):
                pe.wait_ge(ident_ok, 1)
                for g in range(NT // 2):
                    if g >= 2:
                        pe.wait_ge(zt_lo, g - 1)
                    pe.wait_ge(z_done, 2 * g + 2)
                    for i in range(2):
                        for c in range(DT):
                            mm = pe.transpose(bank[g % 2][:, c, i * P:(i + 1) * P], z[(2 * g + i) % 4][:, c * P:(c + 1) * P], T.ident[:])
                    mm.then_inc(zt_done, 1)


CLOSING = [("T", 0, 0), ("T", 0, 1), ("T", 1, 0), ("T", 1, 1), ("W", 0, 0), ("T", 2, 0), ("T", 2, 1), ("W", 1, 0),
           ("T", 3, 0), ("T", 3, 1), ("W", 2, 0), ("W", 3, 0)]
V_GROUPS = QT * (CW // 512)
PAIR_GROUP0 = V_GROUPS
CLOSE_GROUP0 = V_GROUPS + 2 * PAIRS
GROUPS = CLOSE_GROUP0 + len(CLOSING)


def three_products(pe, out, stat, mov, first, last):
    pe.matmul(out, stat[0], mov[0], start=first, stop=False)
    pe.matmul(out, stat[0], mov[1], start=False, stop=False)
    return pe.matmul(out, stat[1], mov[0], start=False, stop=last)


def phase_attention0(nc, sem, T, dram):
    NBUF = 4
    TURN_LAG, ATTEND_LAG = 3, 5
    with ExitStack() as ctx:
        sb, ps = make_tensors(nc, ctx)
        v = Split(sb, "v", [P, QT, CW])
        q = [Split(sb, f"q{i}", [P, S]) for i in range(2)]
        k = [Split(sb, f"k{i}", [P, S]) for i in range(2)]
        o_t = [Split(sb, f"o_t{i}", [P, CT, P]) for i in range(2)]
        o = sb("o", [P, QT, CW])
        masked = [sb(f"masked{i}", [P, S]) for i in range(NBUF)]
        e = [sb(f"e{i}", [P, S]) for i in range(NBUF)]
        e_t = [Split(sb, f"e_t{i}", [P, QT, P]) for i in range(NBUF)]
        mask_raw = sb("mask_raw", [P, QT, S], I32)
        mask_bias = sb("mask_bias", [P, QT, S], BF16)
        neg_max = sb("neg_max", [P, 2, UNITS])
        den = sb("den", [P, 2, UNITS])
        rden = sb("rden", [P, UNITS])
        gate = sb("gate", [1, 2 * UNITS])
        pj = [ps(f"pj{i}", [P, 512]) for i in range(2)]
        sc = [ps(f"sc{i}", [P, S]) for i in range(2)]
        et = [ps(f"et{i}", [P, QT, P]) for i in range(2)]
        ob = [ps(f"ob{i}", [P, UNITS, DK]) for i in range(2)]

        pj_full, pj_hi, pj_split = sem("pj_full"), sem("pj_hi"), sem("pj_split")
        scores, masked_ok, exp_ok = sem("scores"), sem("masked_ok"), sem("exp_ok")
        turned, turned_hi, turned_lo, pv_done = sem("turned"), sem("turned_hi"), sem("turned_lo"), sem("pv_done")
        rden_ok, normed = sem("rden_ok"), sem("normed")
        mask_in, bias_ok = sem("mask_in"), sem("bias_ok")

        def run_pairs(eng, prologue, unit_step, drain, closing):
            with eng.Fori(0, B) as b:
                prologue(b)

                def two_pairs(m, first, last):
                    for par in range(2):
                        for j in range(UNITS):
                            unit_step(b, m, par, j, first and par == 0, last and par == 1)

                two_pairs(0, True, False)
                with eng.Fori(1, PAIRS // 2 - 1) as m:
                    two_pairs(m, False, False)
                two_pairs(PAIRS // 2 - 1, False, True)
                drain(b)
                closing(b)

        def unit(b, m, par, j):
            return b * (PAIRS * UNITS) + m * (2 * UNITS) + (par * UNITS + j)

        def group(b, m, par, which):
            return b * GROUPS + m * 4 + (PAIR_GROUP0 + 2 * (par + 1) + which)

        LAST_M = PAIRS // 2 - 1
        with nc.Block() as block:

            @block.sync
            def _(sp):
                for b in range(B):
                    if b > 0:
                        sp.wait_ge(bias_ok, b)
                    sp.dma_start(mask_raw[:], dram["mask"][b].rearrange("(t p) k -> p t k", p=P)).then_inc(mask_in, 16)

            @block.gpsimd
            def _(pool):
                for b in range(B):
                    pool.wait_ge(mask_in, b * 16 + 16)
                    pool.wait_ge(masked_ok, b * (PAIRS * UNITS) + 2)
                    pool.tensor_scalar(mask_bias[:], mask_raw[:], 0.0, MASKED, ALU.is_equal, ALU.mult).then_inc(bias_ok, 1)

            @block.tensor
            def _(pe):
                def open_group(g, parity):
                    pe.wait_ge(pj_split, g + 1)
                    return pj[parity]

                def project(b, g, parity, w, src_t, col):
                    out = open_group(g, parity)
                    for c in range(DT):
                        mm = three_products(pe, out[:], (w.hi[:, c, bass.ds(col, P)], w.lo[:, c, bass.ds(col, P)]),
                                            (src_t.hi[:, c, bass.ds(b * S, S)], src_t.lo[:, c, bass.ds(b * S, S)]),
                                            c == 0, c == DT - 1)
                    mm.then_inc(pj_full, 1)

                def prologue(b):
                    for n in range(V_GROUPS):
                        kt, half = n // 2, n % 2
                        out = open_group(b * GROUPS + n, n % 2)
                        for c in range(DT):
                            mm = three_products(pe, out[:], (T.ctx_t.hi[:, c, bass.ds(b * S + kt * P, P)], T.ctx_t.lo[:, c, bass.ds(b * S + kt * P, P)]),
                                                (T.wv0.hi[:, c, half * 512:(half + 1) * 512], T.wv0.lo[:, c, half * 512:(half + 1) * 512]),
                                                c == 0, c == DT - 1)
                        mm.then_inc(pj_full, 1)
                    project(b, b * GROUPS + PAIR_GROUP0, 0, T.wq0, T.z_t, 0)
                    project(b, b * GROUPS + PAIR_GROUP0 + 1, 1, T.wk0, T.ctx_t, 0)

                def score(u, b, m, par, j):
                    a, qt = j // QT, j % QT
                    rows = slice(a * DK, (a + 1) * DK)
                    cols = slice(qt * P, (qt + 1) * P)
                    if j == 0:
                        pe.wait_ge(pj_split, group(b, m, par, 1) - 2 + 3)
                    pe.wait_ge(masked_ok, u + 1)
                    three_products(pe, sc[j % 2][:], (q[par].hi[rows, cols], q[par].lo[rows, cols]),
                                   (k[par].hi[rows, :], k[par].lo[rows, :]), True, True).then_inc(scores, 1)

                def turn(u, j):
                    pe.wait_ge(exp_ok, u + (NBUF + 1))
                    pe.wait_ge(turned_lo, u + 1)
                    for kt in range(QT):
                        mm = pe.transpose(et[j % 2][:, kt, :], e[j % NBUF][:, kt * P:(kt + 1) * P], T.ident[:])
                    mm.then_inc(turned, 1)

                def lagged(b, m, par, j, lag):
                    n = par * UNITS + j - lag
                    return (m, n // UNITS, n % UNITS) if n >= 0 else (m - 1, 1, n + 2 * UNITS - UNITS)

                def do_attend(b, m, par, j):
                    u = unit(b, m, par, j)
                    a = j // QT
                    col = m * (2 * P) + (par * P + a * DK)
                    if j == 0:
                        pe.wait_ge(normed, b * PAIRS + m * 2 + (par + 1))
                    pe.wait_ge(turned_lo, u + 3)
                    for kt in range(QT):
                        vv = (v.hi[:, kt, bass.ds(col, DK)], v.lo[:, kt, bass.ds(col, DK)])
                        mm = three_products(pe, ob[par][:, j, :], (e_t[j % NBUF].hi[:, kt, :], e_t[j % NBUF].lo[:, kt, :]), vv, kt == 0, kt == QT - 1)
                    mm.then_inc(pv_done, 1)

                def unit_step(b, m, par, j, first, last):
                    u = unit(b, m, par, j)
                    score(u, b, m, par, j)
                    if not (first and j < TURN_LAG):
                        mm_, pp, jj = lagged(b, m, par, j, TURN_LAG)
                        turn(unit(b, mm_, pp, jj), jj)
                    if not (first and j < ATTEND_LAG):
                        do_attend(b, *lagged(b, m, par, j, ATTEND_LAG))
                    if not last and j == 1:
                        project(b, group(b, m, par, 0), 0, T.wq0, T.z_t, m * (2 * P) + (par + 1) * P)
                    if not last and j == 4:
                        project(b, group(b, m, par, 1), 1, T.wk0, T.ctx_t, m * (2 * P) + (par + 1) * P)

                def drain(b):
                    for j in range(UNITS, UNITS + ATTEND_LAG):
                        if j < UNITS + TURN_LAG:
                            turn(unit(b, LAST_M, 1, j - TURN_LAG), j - TURN_LAG)
                        do_attend(b, LAST_M, 1, j - ATTEND_LAG)

                def closing(b):
                    for i, (what, qt, half) in enumerate(CLOSING):
                        g = b * GROUPS + (CLOSE_GROUP0 + i)
                        out = open_group(g, i % 2)
                        if what == "T":
                            if i == 0:
                                pe.wait_ge(normed, b * PAIRS + (PAIRS + 2))
                            for c in range(4):
                                ct = half * 4 + c
                                mm = pe.transpose(out[:, c * P:(c + 1) * P], o[:, qt, ct * P:(ct + 1) * P], T.ident[:])
                        else:
                            done = CLOSING.index(("T", qt, 1))
                            pe.wait_ge(pj_split, b * GROUPS + (CLOSE_GROUP0 + done) + 3)
                            for ct in range(CT):
                                ot = o_t[qt % 2]
                                mm = three_products(pe, out[:, 0:D], (ot.hi[:, ct, :], ot.lo[:, ct, :]),
                                                    (T.wo0.hi[:, ct, :], T.wo0.lo[:, ct, :]), ct == 0, ct == CT - 1)
                        mm.then_inc(pj_full, 1)

                run_pairs(pe, prologue, unit_step, drain, closing)

            @block.scalar
            def _(act):
                def split_hi(g, parity, dst):
                    act.wait_ge(pj_full, g + 1)
                    nc.scalar.activation(dst, pj[parity][:], ACT.Copy).then_inc(pj_hi, 1)

                def prologue(b):
                    for n in range(V_GROUPS):
                        split_hi(b * GROUPS + n, n % 2, v.hi[:, n // 2, (n % 2) * 512:(n % 2 + 1) * 512])
                    split_hi(b * GROUPS + PAIR_GROUP0, 0, q[0].hi[:])
                    split_hi(b * GROUPS + PAIR_GROUP0 + 1, 1, k[0].hi[:])

                def turned_part(u, j):
                    act.wait_ge(turned, u + 1)
                    act.wait_ge(pv_done, u + 1)
                    nc.scalar.activation(e_t[j % NBUF].hi[:], et[j % 2][:], ACT.Copy).then_inc(turned_hi, 1)

                def unit_step(b, m, par, j, first, last):
                    u = unit(b, m, par, j)
                    if not (first and j < TURN_LAG):
                        turned_part(u - TURN_LAG, (j - TURN_LAG) % UNITS)
                    act.wait_ge(masked_ok, u + 3)
                    if j == 0:
                        act.wait_ge(normed, b * PAIRS + m * 2 + (par + 1))
                    nc.scalar.activation(e[j % NBUF][:], masked[j % NBUF][:], ACT.Exp, bias=neg_max[:, par, j:j + 1], scale=-1.0,
                                         accum_out=den[:, par, j:j + 1]).then_inc(exp_ok, 1)
                    if not last and j == 2:
                        split_hi(group(b, m, par, 0), 0, q[1 - par].hi[:])
                    if not last and j == 5:
                        split_hi(group(b, m, par, 1), 1, k[1 - par].hi[:])

                def drain(b):
                    for j in range(UNITS - TURN_LAG, UNITS):
                        turned_part(unit(b, LAST_M, 1, j), j)

                def closing(b):
                    for i, (what, qt, half) in enumerate(CLOSING):
                        if what == "T":
                            split_hi(b * GROUPS + (CLOSE_GROUP0 + i), i % 2, o_t[qt % 2].hi[:, half * 4:half * 4 + 4, :].rearrange("p c n -> p (c n)"))

                act.sem_inc(pv_done, NBUF)
                act.sem_inc(exp_ok, NBUF)
                run_pairs(act, prologue, unit_step, drain, closing)

            @block.vector
            def _(dve):
                hi_count = [0]

                def split_lo(g, h, parity, hi, lo):
                    dve.wait_ge(pj_hi, h + 1)
                    nc.vector.tensor_tensor(lo, pj[parity][:], hi, ALU.subtract).then_inc(pj_split, 1)

                T_COUNT = V_GROUPS + 2 * PAIRS + sum(w == "T" for w, _, _ in CLOSING)

                def prologue(b):
                    for n in range(V_GROUPS):
                        cols = slice((n % 2) * 512, (n % 2 + 1) * 512)
                        split_lo(None, b * T_COUNT + n, n % 2, v.hi[:, n // 2, cols], v.lo[:, n // 2, cols])
                    split_lo(None, b * T_COUNT + PAIR_GROUP0, 0, q[0].hi[:], q[0].lo[:])
                    split_lo(None, b * T_COUNT + PAIR_GROUP0 + 1, 1, k[0].hi[:], k[0].lo[:])

                def turned_part(u, j):
                    dve.wait_ge(turned_hi, u + 1)
                    nc.vector.tensor_tensor(e_t[j % NBUF].lo[:], et[j % 2][:], e_t[j % NBUF].hi[:], ALU.subtract).then_inc(turned_lo, 1)

                def normalize(b, m, par):
                    u = unit(b, m, par, UNITS - 1)
                    dve.wait_ge(pv_done, u + (NBUF + 1))
                    nc.vector.reciprocal(rden[:], den[:, par, :]).then_inc(rden_ok, 1)
                    dve.wait_ge(rden_ok, b * PAIRS + m * 2 + (par + 1))
                    for a in range(2):
                        col = m * (2 * P) + (par * P + a * DK)
                        op = nc.vector.tensor_tensor(o[:, :, bass.ds(col, DK)], ob[par][:, a * QT:(a + 1) * QT, :],
                                                     rden[:, a * QT:(a + 1) * QT].unsqueeze(2).to_broadcast([P, QT, DK]), ALU.mult)
                    op.then_inc(normed, 1)

                def unit_step(b, m, par, j, first, last):
                    u = unit(b, m, par, j)
                    if first and j == 0:
                        dve.wait_ge(bias_ok, b + 1)
                    dve.wait_ge(scores, u + 1)
                    dve.wait_ge(exp_ok, u + 1)
                    nc.vector.memset(gate[:, par * UNITS + j:par * UNITS + j + 1], 0.0)
                    nc.vector.tensor_tensor_reduce(masked[j % NBUF][:], sc[j % 2][:], mask_bias[:, j % QT, :],
                                                   -SCALE0, 3e38, ALU.add, ALU.min, neg_max[:, par, j:j + 1]).then_inc(masked_ok, 1)
                    if not (first and j < TURN_LAG):
                        turned_part(u - TURN_LAG, (j - TURN_LAG) % UNITS)
                    if not last and j == 2:
                        split_lo(None, b * T_COUNT + m * 4 + (PAIR_GROUP0 + 2 * (par + 1)), 0, q[1 - par].hi[:], q[1 - par].lo[:])
                    if not last and j == 5:
                        split_lo(None, b * T_COUNT + m * 4 + (PAIR_GROUP0 + 2 * (par + 1) + 1), 1, k[1 - par].hi[:], k[1 - par].lo[:])
                    if j == ATTEND_LAG + 1 and not first:
                        if par == 1:
                            normalize(b, m, 0)
                        else:
                            normalize(b, m - 1, 1)

                def drain(b):
                    for j in range(UNITS - TURN_LAG, UNITS):
                        turned_part(unit(b, LAST_M, 1, j), j)
                    normalize(b, LAST_M, 1)

                def closing(b):
                    n = V_GROUPS + 2 * PAIRS
                    for i, (what, qt, half) in enumerate(CLOSING):
                        if what == "T":
                            ot = o_t[qt % 2]
                            split_lo(None, b * T_COUNT + n, i % 2, ot.hi[:, half * 4:half * 4 + 4, :].rearrange("p c n -> p (c n)"),
                                     ot.lo[:, half * 4:half * 4 + 4, :].rearrange("p c n -> p (c n)"))
                            n += 1
                        else:
                            dve.wait_ge(pj_full, b * GROUPS + (CLOSE_GROUP0 + i + 1))
                            xt = T.x[:, bass.ds(b * QT + qt, 1), :].rearrange("p o d -> p (o d)")
                            nc.vector.tensor_tensor(xt, pj[i % 2][:, 0:D], xt, ALU.add).then_inc(pj_split, 1)

                dve.sem_inc(pj_split, 2)
                dve.sem_inc(masked_ok, 2)
                dve.sem_inc(turned_lo, 2)
                dve.sem_inc(normed, 2)
                run_pairs(dve, prologue, unit_step, drain, closing)


EXPERTS0 = 8
FF0 = 4 * D
FT0 = FF0 // P
CAP = B * S // EXPERTS0
HALVES = CAP // P
DIGITS = 13
CANDS = 3


def prefix_counts(pe, out, flags, tri, ones, zeros, cols):
    pe.matmul(out, tri[:], flags[:], start=True, stop=False)
    for t in range(NT - 1):
        pe.matmul(out[:, t + 1:, :], ones[:], flags[:, t:t + 1, :].to_broadcast([P, NT - 1 - t, cols]), start=False, stop=False)
    return pe.matmul(out, ones[:], zeros[:], start=False, stop=True)


def phase_route0(nc, sem, T, dram):
    with ExitStack() as ctx:
        sb, ps = make_tensors(nc, ctx)
        stats, mv, sd, rstd = sb("r_stats", [P, NT, 6]), sb("r_mv", [P, NT, 2]), sb("r_sd", [P, NT]), sb("r_rstd", [P, NT])
        xf, y = sb("r_xf", [P, NT, D]), sb("r_y", [P, NT, D])
        xf_t = sb("r_xf_t", [P, DT, B * S])
        gate = sb("r_gate", [P, DT, EXPERTS0])
        score = sb("r_score", [P, NT, EXPERTS0])
        ones, tri = sb("r_ones", [P, P], F16), sb("r_tri", [P, P], F16)
        zeros = sb("r_zeros", [P, NT, EXPERTS0], F16)
        flags = sb("r_flags", [P, NT, CANDS, EXPERTS0], F16)
        base = [sb(f"r_base{i}", [P, EXPERTS0]) for i in range(2)]
        step = [sb(f"r_step{i}", [P, 1]) for i in range(2)]
        offs, cand = sb("r_offs", [P, CANDS, EXPERTS0]), sb("r_cand", [P, CANDS, EXPERTS0])
        met, nmet = sb("r_met", [P, CANDS, EXPERTS0]), sb("r_nmet", [P, EXPERTS0])
        above, equal, chosen = (sb(n, [P, NT, EXPERTS0], F16) for n in ("r_above", "r_equal", "r_chosen"))
        need, tie = sb("r_need", [P, EXPERTS0]), sb("r_tie", [P, NT, EXPERTS0], F16)
        place = sb("r_place", [P, NT, EXPERTS0])
        iota_f, iota16, ids = sb("r_iota_f", [P, CAP]), sb("r_iota16", [P, CAP], F16), sb("r_ids", [P, NT])
        vals = sb("r_vals", [P, NT, EXPERTS0, 3], F16)
        hot = [sb(f"r_hot{i}", [P, CAP], F16) for i in range(8)]
        got = sb("r_got", [P, EXPERTS0, HALVES, 3])
        tb = [ps(f"r_tb{i}", [P, DT, 2 * P]) for i in range(2)]
        banks = [ps(f"r_bank{i}", [P, 512]) for i in range(3)]
        sp_ = banks[0][:, 0:NT * EXPERTS0].rearrange("p (t e) -> p t e", e=EXPERTS0)
        cp = banks[1][:, 0:CANDS * EXPERTS0].rearrange("p (c e) -> p c e", e=EXPERTS0)
        pp = banks[2][:, 0:NT * EXPERTS0].rearrange("p (t e) -> p t e", e=EXPERTS0)
        slots = [ps(f"r_slots{i}", [P, 512]) for i in range(HALVES)]

        (gate_in, rstd_done, xf_done, sum_done, y_done, stored_y, stored_s, turned, copied,
         logits, tanh_ok, consts, v, searched, counted, prefixed, hot_ok, listed) = (sem("r" + n) for n in (
             "gate_in", "rstd_done", "xf_done", "sum_done", "y_done", "stored_y", "stored_s",
             "turned", "copied", "logits", "tanh_ok", "consts", "v", "searched", "counted", "prefixed", "hot_ok", "listed"))
        tri_set = sem("rtri_set")
        with nc.Block() as block:

            @block.sync
            def _(sp):
                sp.dma_start(gate[:], dram["gate0"].rearrange("(c p) e -> p c e", p=P)).then_inc(gate_in, 16)
                sp.wait_ge(sum_done, 1)
                sp.dma_start(dram["acc"].rearrange("(t p) d -> p t d", p=P), T.x[:]).then_inc(stored_s, 16)
                sp.wait_ge(y_done, NT)
                sp.dma_start(dram["y"].rearrange("(t p) d -> p t d", p=P), y[:]).then_inc(stored_y, 16)
                sp.wait_ge(stored_s, 16)
                sp.wait_ge(stored_y, 16)

            @block.gpsimd
            def _(pool):
                pool.memset(zeros[:], 0.0)
                pool.memset(ones[:], 1.0).then_inc(tri_set, 1)
                pool.wait_ge(tri_set, 1)
                pool.affine_select(out=tri[:], in_=ones[:], compare_op=ALU.is_gt, fill=0.0, base=0,
                                   pattern=[[1, P]], channel_multiplier=-1).then_inc(consts, 1)
                pool.iota(iota_f[:], pattern=[[1, CAP]], base=1, channel_multiplier=0, allow_small_or_imprecise_dtypes=True).then_inc(consts, 1)
                pool.iota(ids[:], pattern=[[P, NT]], base=0, channel_multiplier=1, allow_small_or_imprecise_dtypes=True).then_inc(consts, 1)
                for c in range(CANDS):
                    pool.memset(offs[:, c, :], float(c + 1)).then_inc(consts, 1)
                pool.wait_ge(consts, 3 + CANDS)
                pool.tensor_copy(iota16[:], iota_f[:]).then_inc(consts, 1)
                for e in range(EXPERTS0):
                    pool.tensor_copy(vals[:, :, e, 0], ids[:]).then_inc(consts, 1)
                pool.wait_ge(xf_done, NT)
                pool.tensor_tensor(T.x[:], T.x[:], xf[:], ALU.add).then_inc(sum_done, 1)

            @block.scalar
            def _(act):
                layernorm_root(nc, act, T, 1, sd)
                layernorm_root(nc, act, T, 2, sd)
                for g in range(NT // 2):
                    act.wait_ge(turned, g + 1)
                    nc.scalar.activation(xf_t[:, :, g * 2 * P:(g + 1) * 2 * P], tb[g % 2][:], ACT.Copy).then_inc(copied, 1)
                act.wait_ge(logits, 1)
                nc.scalar.activation(score[:], sp_, ACT.Tanh).then_inc(tanh_ok, 1)

            @block.tensor
            def _(pe):
                for g in range(NT // 2):
                    if g >= 2:
                        pe.wait_ge(copied, g - 1)
                    pe.wait_ge(xf_done, 2 * g + 2)
                    for i in range(2):
                        for c in range(DT):
                            mm = pe.transpose(tb[g % 2][:, c, i * P:(i + 1) * P], xf[:, 2 * g + i, c * P:(c + 1) * P], T.ident[:])
                    mm.then_inc(turned, 1)
                pe.wait_ge(gate_in, 16)
                pe.wait_ge(copied, NT // 2)
                for t in range(NT):
                    for c in range(DT):
                        mm = pe.matmul(sp_[:, t, :], xf_t[:, c, t * P:(t + 1) * P], gate[:, c, :], start=(c == 0), stop=(c == DT - 1))
                mm.then_inc(logits, 1)
                pe.wait_ge(consts, 1)
                with pe.Fori(0, DIGITS) as r:
                    pe.wait_ge(searched, r + 1)
                    for t in range(NT):
                        mm = pe.matmul(cp, ones[:], flags[:, t, :, :], start=(t == 0), stop=(t == NT - 1))
                    mm.then_inc(counted, 1)
                pe.wait_ge(searched, DIGITS + 1)
                for t in range(NT):
                    mm = pe.matmul(cp[:, 0, :], ones[:], above[:, t, :], start=(t == 0), stop=(t == NT - 1))
                mm.then_inc(counted, 1)
                prefix_counts(pe, pp, equal, tri, ones, zeros, EXPERTS0).then_inc(prefixed, 1)
                pe.wait_ge(searched, DIGITS + 2)
                prefix_counts(pe, pp, chosen, tri, ones, zeros, EXPERTS0).then_inc(prefixed, 1)
                for e in range(EXPERTS0):
                    for t in range(NT):
                        n = e * NT + t
                        pe.wait_ge(hot_ok, n + 1)
                        for h in range(HALVES):
                            mm = pe.matmul(slots[h][:, 4 * e:4 * e + 3], hot[n % 8][:, h * P:(h + 1) * P], vals[:, t, e, :],
                                           start=(t == 0), stop=(t == NT - 1))
                        mm.then_inc(listed, 1)

            @block.vector
            def _(dve):
                steps = [0]

                def step_done(op):
                    steps[0] += 1
                    op.then_inc(v, 1)
                    dve.wait_ge(v, steps[0])

                layernorm_stats(nc, dve, T, 1, T.x, stats, mv, sd)
                step_done(nc.vector.reciprocal(rstd[:], sd[:]))
                for t in range(NT):
                    nc.vector.tensor_scalar(xf[:, t, :], T.x[:, t, :], mv[:, t, 0:1], rstd[:, t:t + 1], ALU.subtract, ALU.mult).then_inc(xf_done, 1)
                dve.wait_ge(xf_done, NT)
                layernorm_stats(nc, dve, T, 2, xf, stats, mv, sd)
                step_done(nc.vector.reciprocal(rstd[:], sd[:]))
                for t in range(NT):
                    nc.vector.tensor_scalar(y[:, t, :], xf[:, t, :], mv[:, t, 0:1], rstd[:, t:t + 1], ALU.subtract, ALU.mult).then_inc(y_done, 1)
                dve.wait_ge(tanh_ok, 1)
                step_done(nc.vector.tensor_scalar(score[:], score[:], 1.0, 0.5, ALU.add, ALU.mult))
                nc.vector.memset(base[0][:], 0.0)
                step_done(nc.vector.memset(step[0][:], 0.25))
                dve.wait_ge(consts, 3 + CANDS)
                step_done(nc.vector.tensor_scalar(cand[:], offs[:], 0.25, None, ALU.mult))
                first = steps[0]
                per_round = 5

                def digit(r, i):
                    v0 = r * per_round + first
                    nc.vector.tensor_tensor(flags[:], score[:].unsqueeze(2).to_broadcast([P, NT, CANDS, EXPERTS0]),
                                            cand[:].unsqueeze(1).to_broadcast([P, NT, CANDS, EXPERTS0]), ALU.is_ge).then_inc(searched, 1)
                    nc.vector.tensor_scalar(step[1 - i][:], step[i][:], 0.25, None, ALU.mult).then_inc(v, 1)
                    dve.wait_ge(counted, r + 1)
                    nc.vector.tensor_scalar(met[:], cp, float(CAP), None, ALU.is_ge).then_inc(v, 1)
                    dve.wait_ge(v, v0 + 2)
                    nc.vector.tensor_reduce(nmet[:], met[:].rearrange("p c e -> p e c"), AX.X, ALU.add).then_inc(v, 1)
                    dve.wait_ge(v, v0 + 3)
                    nc.vector.scalar_tensor_tensor(out=base[1 - i][:], in0=nmet[:], scalar=step[i][:, 0:1], in1=base[i][:],
                                                   op0=ALU.mult, op1=ALU.add).then_inc(v, 1)
                    dve.wait_ge(v, v0 + 4)
                    nc.vector.scalar_tensor_tensor(out=cand[:], in0=offs[:], scalar=step[1 - i][:, 0:1],
                                                   in1=base[1 - i][:].unsqueeze(1).to_broadcast([P, CANDS, EXPERTS0]),
                                                   op0=ALU.mult, op1=ALU.add).then_inc(v, 1)
                    dve.wait_ge(v, v0 + 5)

                digit(0, 0)
                with dve.Fori(0, DIGITS // 2) as rr:
                    digit(rr * 2 + 1, 1)
                    digit(rr * 2 + 2, 0)
                steps[0] = first + per_round * DIGITS
                kth = base[1][:].unsqueeze(1).to_broadcast([P, NT, EXPERTS0])
                nc.vector.tensor_tensor(above[:], score[:], kth, ALU.is_gt).then_inc(v, 1)
                steps[0] += 1
                nc.vector.tensor_tensor(equal[:], score[:], kth, ALU.is_equal).then_inc(searched, 1)
                nc.vector.tensor_copy(vals[:, :, :, 1], score[:]).then_inc(v, 1)
                steps[0] += 1
                dve.wait_ge(v, steps[0])
                step_done(nc.vector.tensor_tensor(vals[:, :, :, 2], score[:], vals[:, :, :, 1], ALU.subtract))
                dve.wait_ge(counted, DIGITS + 1)
                step_done(nc.vector.tensor_scalar(need[:], cp[:, 0, :], -1.0, float(CAP), ALU.mult, ALU.add))
                dve.wait_ge(prefixed, 1)
                step_done(nc.vector.tensor_tensor(tie[:], pp, need[:].unsqueeze(1).to_broadcast([P, NT, EXPERTS0]), ALU.is_lt))
                step_done(nc.vector.tensor_tensor(tie[:], tie[:], equal[:], ALU.mult))
                nc.vector.tensor_tensor(chosen[:], tie[:], above[:], ALU.add).then_inc(searched, 1)
                dve.wait_ge(searched, DIGITS + 2)
                dve.wait_ge(prefixed, 2)
                step_done(nc.vector.scalar_tensor_tensor(out=place[:], in0=pp, scalar=1.0, in1=chosen[:], op0=ALU.add, op1=ALU.mult))
                dve.wait_ge(consts, 4 + CANDS + EXPERTS0)
                for e in range(EXPERTS0):
                    for t in range(NT):
                        n = e * NT + t
                        if n >= 8:
                            dve.wait_ge(listed, n - 7)
                        nc.vector.tensor_scalar(hot[n % 8][:], iota16[:], place[:, t, e:e + 1], None, ALU.is_equal).then_inc(hot_ok, 1)
                dve.wait_ge(listed, EXPERTS0 * NT)
                for h in range(HALVES):
                    op = nc.vector.tensor_copy(got[:, :, h, :], slots[h][:, 0:4 * EXPERTS0].rearrange("p (e c) -> p e c", c=4)[:, :, 0:3])
                step_done(op)
                nc.vector.tensor_copy(T.slot_token[:], got[:, :, :, 0])
                step_done(nc.vector.tensor_tensor(T.slot_weight[:], got[:, :, :, 1], got[:, :, :, 2], ALU.add))


def phase_experts0(nc, sem, T, dram):
    with ExitStack() as ctx:
        sb, ps = make_tensors(nc, ctx)
        raw1 = [sb(f"raw1_{i}", [P, DT, FF0]) for i in range(2)]
        raw2 = [sb(f"raw2_{i}", [P, FT0, D]) for i in range(2)]
        w1 = [Split(sb, f"w1_{i}", [P, DT, FF0]) for i in range(2)]
        w2 = [Split(sb, f"w2_{i}", [P, FT0, D]) for i in range(2)]
        bias1, bias2 = sb("bias1", [P, EXPERTS0, FT0]), sb("bias2", [P, EXPERTS0, D])
        gamma, beta = sb("gamma", [P, DT]), sb("beta", [P, DT])
        yg = [sb(f"yg{i}", [P, HALVES, D]) for i in range(2)]
        yt = [sb(f"yt{i}", [P, DT, CAP]) for i in range(2)]
        yts = [Split(sb, f"yts{i}", [P, DT, CAP]) for i in range(2)]
        h = [sb(f"h{i}", [P, 2, CAP]) for i in range(2)]
        hs = [Split(sb, f"hs{i}", [P, FT0, CAP]) for i in range(2)]
        wb2 = [sb(f"wb2_{i}", [P, HALVES, D]) for i in range(2)]
        res = [sb(f"res{i}", [P, HALVES, D]) for i in range(2)]
        tb = [ps(f"f_tb{i}", [P, DT, CAP]) for i in range(2)]
        hb = [ps(f"f_hb{i}", [P, 2, CAP]) for i in range(2)]
        ob = [ps(f"f_ob{i}", [P, HALVES, D]) for i in range(2)]
        GR = FT0 // 2
        (small_in, gathered0, gathered1, raw1_in0, raw1_in1, raw2_in0, raw2_in1, w1_hi, w1_lo, w2_hi, w2_lo, turned, affine, y_hi, y_lo, h_full, h_act, h_hi, h_lo,
         fc2_done, wb2_ok, res_ok, res_free, added) = (sem("f" + n) for n in (
             "small_in", "gathered0", "gathered1", "raw1_in0", "raw1_in1", "raw2_in0", "raw2_in1", "w1_hi", "w1_lo", "w2_hi", "w2_lo", "turned", "affine", "y_hi", "y_lo", "h_full",
             "h_act", "h_hi", "h_lo", "fc2_done", "wb2_ok", "res_ok", "res_free", "added"))
        gathered, raw1_in, raw2_in = (gathered0, gathered1), (raw1_in0, raw1_in1), (raw2_in0, raw2_in1)
        E = EXPERTS0

        def run_experts(eng, head, tail):
            head(0, 0)
            with eng.Fori(0, E // 2 - 1) as m:
                head(m * 2 + 1, 1)
                tail(m * 2, 0)
                head(m * 2 + 2, 0)
                tail(m * 2 + 1, 1)
            head(E - 1, 1)
            tail(E - 2, 0)
            tail(E - 1, 1)

        with nc.Block() as block:

            @block.sync
            def _(sp):
                def load1(e):
                    if e >= 2:
                        sp.wait_ge(w1_lo, e - 1)
                    sp.dma_start(raw1[e % 2][:], dram["fc1"][e].rearrange("(c p) f -> p c f", p=P)).then_inc(raw1_in[e % 2], 16)

                def load2(e):
                    if e >= 2:
                        sp.wait_ge(w2_lo, e - 1)
                    sp.dma_start(raw2[e % 2][:], dram["fc2"][e].rearrange("(c p) d -> p c d", p=P)).then_inc(raw2_in[e % 2], 16)

                load1(0)
                sp.dma_start(gamma[:], dram["gamma"]).then_inc(small_in, 16)
                sp.dma_start(beta[:], dram["beta"]).then_inc(small_in, 16)
                sp.dma_start(bias1[:], dram["b1"]).then_inc(small_in, 16)
                sp.dma_start(bias2[:], dram["b2"].unsqueeze(0).to_broadcast([P, E, D])).then_inc(small_in, 16)
                for e in range(1, E):
                    load1(e)
                    load2(e - 1)
                load2(E - 1)

            @block.gpsimd
            def _(pool):
                def gather(e):
                    if e >= 2:
                        pool.wait_ge(turned, e - 1)
                    for n in range(HALVES):
                        pool.indirect_dma_start(out=yg[e % 2][:, n, :], out_offset=None, in_=dram["y"],
                                                in_offset=bass.IndirectOffsetOnAxis(ap=T.slot_token[:, e, n:n + 1], axis=0)).then_inc(gathered[e % 2], 16)

                def split1(e):
                    pool.wait_ge(w1_hi, e + 1)
                    pool.tensor_tensor(w1[e % 2].lo[:], raw1[e % 2][:], w1[e % 2].hi[:], ALU.subtract).then_inc(w1_lo, 1)

                def split2(e):
                    pool.wait_ge(w2_hi, e + 1)
                    pool.tensor_tensor(w2[e % 2].lo[:], raw2[e % 2][:], w2[e % 2].hi[:], ALU.subtract).then_inc(w2_lo, 1)

                def weigh_bias(e):
                    pool.wait_ge(res_ok, e + 1)
                    for n in range(HALVES):
                        op = pool.tensor_scalar(wb2[e % 2][:, n, :], bias2[:, e, :], T.slot_weight[:, e, n:n + 1], None, ALU.mult)
                    op.then_inc(wb2_ok, 1)

                def scatter(e):
                    pool.wait_ge(res_ok, e + 3)
                    if e >= 1:
                        pool.wait_ge(added, e * 16 * HALVES)
                        pool.sem_inc(res_free, 1)
                    for n in range(HALVES):
                        pool.indirect_dma_start(out=dram["acc"], out_offset=bass.IndirectOffsetOnAxis(ap=T.slot_token[:, e, n:n + 1], axis=0),
                                                in_=res[e % 2][:, n, :], in_offset=None, compute_op=ALU.add).then_inc(added, 16)

                pool.sem_inc(res_free, 2)
                gather(0)
                split1(0)
                gather(1)
                pool.wait_ge(small_in, 64)
                for e in range(E):
                    if e + 1 < E:
                        split1(e + 1)
                    split2(e)
                    if e + 2 < E:
                        gather(e + 2)
                    weigh_bias(e)
                    if e >= 1:
                        scatter(e - 1)
                scatter(E - 1)
                pool.wait_ge(added, E * 16 * HALVES)

            @block.scalar
            def _(act):
                def head(e, i):
                    act.wait_ge(affine, e + 3)
                    nc.scalar.activation(yts[i].hi[:], yt[i][:], ACT.Copy).then_inc(y_hi, 1)
                    for g in range(GR):
                        act.wait_ge(h_full, e * GR + (g + 1))
                        act.wait_ge(h_lo, e * GR + (g + 1))
                        for n in range(2):
                            f = 2 * g + n
                            op = nc.scalar.activation(h[g % 2][:, n, :], hb[g % 2][:, n, :], ACT.Gelu_apprx_tanh,
                                                      bias=bias_at(e, f))
                        op.then_inc(h_act, 1)
                        act.wait_ge(h_act, e * GR + (g + 3))
                        if g == 0:
                            act.wait_ge(fc2_done, e + 1)
                        nc.scalar.activation(hs[i].hi[:, 2 * g:2 * g + 2, :], h[g % 2][:], ACT.Copy).then_inc(h_hi, 1)

                def bias_at(e, f):
                    if isinstance(e, int):
                        return bias1[:, e, f:f + 1]
                    return bias1[:, bass.ds(e, 1), f]

                def weights1(e, i):
                    act.wait_ge(raw1_in[i], (e - i) * 8 + 16)
                    if not isinstance(e, int):
                        act.wait_ge(h_full, e * GR - GR)
                    nc.scalar.activation(w1[i].hi[:], raw1[i][:], ACT.Copy).then_inc(w1_hi, 1)

                def weights2(e, i):
                    act.wait_ge(raw2_in[i], (e - i) * 8 + 16)
                    act.wait_ge(fc2_done, e + 1)
                    nc.scalar.activation(w2[i].hi[:], raw2[i][:], ACT.Copy).then_inc(w2_hi, 1)

                act.sem_inc(h_act, 2)
                act.wait_ge(small_in, 64)
                weights1(0, 0)
                weights1(1, 1)
                head(0, 0)
                weights2(0, 0)
                with act.Fori(0, E // 2 - 1) as m:
                    weights1(m * 2 + 2, 0)
                    head(m * 2 + 1, 1)
                    weights2(m * 2 + 1, 1)
                    weights1(m * 2 + 3, 1)
                    head(m * 2 + 2, 0)
                    weights2(m * 2 + 2, 0)
                head(E - 1, 1)
                weights2(E - 1, 1)

            @block.vector
            def _(dve):
                def head(e, i):
                    dve.wait_ge(turned, e + 1)
                    for c in range(DT):
                        op = nc.vector.tensor_scalar(yt[i][:, c, :], tb[i][:, c, :], gamma[:, c:c + 1], beta[:, c:c + 1], ALU.mult, ALU.add)
                    op.then_inc(affine, 1)
                    dve.wait_ge(y_hi, e + 1)
                    nc.vector.tensor_tensor(yts[i].lo[:], yt[i][:], yts[i].hi[:], ALU.subtract).then_inc(y_lo, 1)
                    for g in range(GR):
                        dve.wait_ge(h_hi, e * GR + (g + 1))
                        nc.vector.tensor_tensor(hs[i].lo[:, 2 * g:2 * g + 2, :], h[g % 2][:], hs[i].hi[:, 2 * g:2 * g + 2, :], ALU.subtract).then_inc(h_lo, 1)

                def tail(e, i):
                    dve.wait_ge(fc2_done, e + 3)
                    dve.wait_ge(wb2_ok, e + 1)
                    dve.wait_ge(res_free, e + 1)
                    for n in range(HALVES):
                        weight = T.slot_weight[:, e, n:n + 1] if isinstance(e, int) else T.slot_weight[:, bass.ds(e, 1), n]
                        op = nc.vector.scalar_tensor_tensor(out=res[i][:, n, :], in0=ob[i][:, n, :], scalar=weight,
                                                            in1=wb2[i][:, n, :], op0=ALU.mult, op1=ALU.add)
                    op.then_inc(res_ok, 1)

                dve.sem_inc(h_lo, 2)
                dve.sem_inc(affine, 2)
                dve.sem_inc(res_ok, 2)
                dve.wait_ge(small_in, 64)
                run_experts(dve, head, tail)

            @block.tensor
            def _(pe):
                def head(e, i):
                    pe.wait_ge(affine, e + 1)
                    pe.wait_ge(gathered[i], (e - i) * (8 * HALVES) + 16 * HALVES)
                    for n in range(HALVES):
                        for c in range(DT):
                            mm = pe.transpose(tb[i][:, c, n * P:(n + 1) * P], yg[i][:, n, c * P:(c + 1) * P], T.ident[:])
                    mm.then_inc(turned, 1)
                    pe.wait_ge(w1_lo, e + 1)
                    pe.wait_ge(y_lo, e + 1)
                    for g in range(GR):
                        pe.wait_ge(h_act, e * GR + (g + 1))
                        for n in range(2):
                            f = 2 * g + n
                            for c in range(DT):
                                mm = three_products(pe, hb[g % 2][:, n, :], (w1[i].hi[:, c, f * P:(f + 1) * P], w1[i].lo[:, c, f * P:(f + 1) * P]),
                                                    (yts[i].hi[:, c, :], yts[i].lo[:, c, :]), c == 0, c == DT - 1)
                        mm.then_inc(h_full, 1)

                def tail(e, i):
                    pe.wait_ge(h_lo, e * GR + (GR + 2))
                    pe.wait_ge(w2_lo, e + 1)
                    pe.wait_ge(res_ok, e + 1)
                    for n in range(HALVES):
                        for f in range(FT0):
                            mm = three_products(pe, ob[i][:, n, :], (hs[i].hi[:, f, n * P:(n + 1) * P], hs[i].lo[:, f, n * P:(n + 1) * P]),
                                                (w2[i].hi[:, f, :], w2[i].lo[:, f, :]), f == 0, f == FT0 - 1)
                    mm.then_inc(fc2_done, 1)

                pe.sem_inc(fc2_done, 2)
                run_experts(pe, head, tail)


DH = D // HEADS
STACK = 4 * DH
SCALE1 = DH ** -0.5
OUTSIDE = -1e30
BAND = P


def window(qt):
    first = max(qt - 1, 0)
    return first, min(qt + 1, QT - 1) - first + 1


def phase_project1(nc, sem, T, dram):
    with ExitStack() as ctx:
        sb, ps = make_tensors(nc, ctx)
        stats, mv, sd, rstd = sb("c_stats", [P, NT, 6]), sb("c_mv", [P, NT, 2]), sb("c_sd", [P, NT]), sb("c_rstd", [P, NT])
        z = [sb(f"c_z{i}", [P, D]) for i in range(4)]
        z_t = Split(sb, "c_z_t", [P, DT, B * S])
        raw = sb("c_raw", [P, 4, DT, D])
        w = Split(sb, "c_w", [P, 4, DT, D])
        bqk, bv, bo = sb("c_bqk", [P, 2, DT]), sb("c_bv", [P, D]), sb("c_bo", [P, D])
        qk = [Split(sb, f"c_qk{i}", [P, S]) for i in range(4)]
        tb = [ps(f"c_tb{i}", [P, DT, 2 * P]) for i in range(2)]
        pb = [ps(f"c_pb{i}", [P, 512]) for i in range(2)]
        names = ("x_in", "w_in", "b_in", "rstd_done", "z_done", "turned", "z_hi", "z_lo", "w_hi", "w_lo",
                 "proj", "qk_hi", "qk_lo", "v_ready", "bo_added")
        (x_in, w_in, b_in, rstd_done, z_done, turned, z_hi, z_lo, w_hi, w_lo,
         proj, qk_hi, qk_lo, v_ready, bo_added) = (sem("c" + n) for n in names)
        v_sum = [sb(f"c_v_sum{i}", [P, 2, D]) for i in range(2)]
        v_hi, v_split = sem("cv_hi"), sem("cv_split")
        stacked = [sem(f"cstacked{i}") for i in range(4)]
        QK = [(b, which, g) for b in range(B) for which in range(2) for g in range(DT)]
        nqk = len(QK)
        NV = NT // 2

        with nc.Block() as block:

            @block.sync
            def _(sp):
                sp.dma_start(T.x[:], dram["acc"].rearrange("(t p) d -> p t d", p=P)).then_inc(x_in, 16)
                for i, name in enumerate(("wq1", "wk1", "wv1", "wo1")):
                    sp.dma_start(raw[:, i, :, :], dram[name].rearrange("(c p) n -> p c n", p=P)).then_inc(w_in, 16)
                for dst, name in ((bqk[:, 0, :], "bq1"), (bqk[:, 1, :], "bk1")):
                    sp.dma_start(dst, dram[name]).then_inc(b_in, 16)
                for dst, name in ((bv, "bv1"), (bo, "bo1")):
                    sp.dma_start(dst[:], dram[name].unsqueeze(0).to_broadcast([P, D])).then_inc(b_in, 16)
                for n, (b, which, g) in enumerate(QK):
                    sp.wait_ge(qk_lo, n + 1)
                    part = qk[n % 4]
                    rows = (part.hi, part.hi, part.lo, part.lo) if which == 0 else (part.hi, part.lo, part.hi, part.lo)
                    heads = HEADS // DT
                    for r, src in enumerate(rows):
                        dst = dram["stack"][which, b, r * DH:(r + 1) * DH, g * heads:(g + 1) * heads, :].rearrange("c h t -> h c t")
                        sp.dma_start(dst, src[:]).then_inc(stacked[n % 4], 16)
                for i in range(4):
                    sp.wait_ge(stacked[i], 64 * (nqk // 4))

            @block.gpsimd
            def _(pool):
                pool.memset(T.band[:], 0.0).then_inc(bo_added, 1)
                pool.wait_ge(bo_added, 1)
                pool.affine_select(out=T.band[:], in_=T.band[:], compare_op=ALU.is_ge, fill=OUTSIDE, base=0,
                                   pattern=[[1, 3 * P]], channel_multiplier=-1).then_inc(bo_added, 1)
                pool.wait_ge(bo_added, 2)
                pool.affine_select(out=T.band[:], in_=T.band[:], compare_op=ALU.is_ge, fill=OUTSIDE, base=2 * BAND,
                                   pattern=[[-1, 3 * P]], channel_multiplier=1).then_inc(bo_added, 1)
                pool.wait_ge(w_hi, 1)
                pool.tensor_tensor(w.lo[:], raw[:], w.hi[:], ALU.subtract).then_inc(w_lo, 1)
                pool.wait_ge(z_done, NT)
                pool.wait_ge(b_in, 64)
                pool.tensor_tensor(T.x[:], T.x[:], bo[:].unsqueeze(1).to_broadcast([P, NT, D]), ALU.add).then_inc(bo_added, 1)

            @block.scalar
            def _(act):
                act.wait_ge(w_in, 64)
                nc.scalar.activation(w.hi[:], raw[:], ACT.Copy).then_inc(w_hi, 1)
                layernorm_root(nc, act, T, 3, sd)
                for g in range(NT // 2):
                    act.wait_ge(turned, g + 1)
                    nc.scalar.activation(z_t.hi[:, :, g * 2 * P:(g + 1) * 2 * P], tb[g % 2][:], ACT.Copy).then_inc(z_hi, 1)
                act.wait_ge(b_in, 64)
                for n, (b, which, g) in enumerate(QK):
                    act.wait_ge(proj, n + 1)
                    if n >= 4:
                        act.wait_ge(stacked[n % 4], 64 * (n // 4))
                    nc.scalar.activation(qk[n % 4].hi[:], pb[n % 2][:], ACT.Identity, bias=bqk[:, which, g:g + 1]).then_inc(qk_hi, 1)
                for n in range(NV):
                    act.wait_ge(v_ready, n + 1)
                    nc.scalar.activation(T.v1[:, 2 * n:2 * n + 2, :, 0, :], v_sum[n % 2][:].rearrange("p t (h d) -> p t h d", d=DH), ACT.Copy).then_inc(v_hi, 1)

            @block.vector
            def _(dve):
                dve.wait_ge(x_in, 16)
                layernorm_stats(nc, dve, T, 3, T.x, stats, mv, sd)
                nc.vector.reciprocal(rstd[:], sd[:]).then_inc(rstd_done, 1)
                dve.wait_ge(rstd_done, 1)

                def lo_part(g):
                    dve.wait_ge(z_hi, g + 1)
                    cols = slice(g * 2 * P, (g + 1) * 2 * P)
                    nc.vector.tensor_tensor(z_t.lo[:, :, cols], tb[g % 2][:], z_t.hi[:, :, cols], ALU.subtract).then_inc(z_lo, 1)

                for t in range(NT):
                    if t >= 4:
                        dve.wait_ge(turned, (t - 4) // 2 + 1)
                    nc.vector.tensor_scalar(z[t % 4][:], T.x[:, t, :], mv[:, t, 0:1], rstd[:, t:t + 1], ALU.subtract, ALU.mult).then_inc(z_done, 1)
                    if t % 2 == 1 and t >= 3:
                        lo_part(t // 2 - 1)
                lo_part(NT // 2 - 1)
                for n, (b, which, g) in enumerate(QK):
                    dve.wait_ge(qk_hi, n + 1)
                    nc.vector.scalar_tensor_tensor(out=qk[n % 4].lo[:], in0=pb[n % 2][:], scalar=bqk[:, which, g:g + 1], in1=qk[n % 4].hi[:],
                                                   op0=ALU.add, op1=ALU.subtract).then_inc(qk_lo, 1)
                dve.wait_ge(b_in, 64)
                for n in range(NV):
                    dve.wait_ge(proj, nqk + n + 1)
                    if n >= 2:
                        dve.wait_ge(v_split, n - 1)
                    nc.vector.tensor_tensor(v_sum[n % 2][:], pb[n % 2][:].rearrange("p (t d) -> p t d", d=D),
                                            bv[:].unsqueeze(1).to_broadcast([P, 2, D]), ALU.add).then_inc(v_ready, 1)
                    dve.wait_ge(v_hi, n + 1)
                    hi, lo = (T.v1[:, 2 * n:2 * n + 2, :, w, :] for w in range(2))
                    nc.vector.tensor_tensor(lo, v_sum[n % 2][:].rearrange("p t (h d) -> p t h d", d=DH), hi, ALU.subtract).then_inc(v_split, 1)

            @block.tensor
            def _(pe):
                for g in range(NT // 2):
                    if g >= 2:
                        pe.wait_ge(z_lo, g - 1)
                    pe.wait_ge(z_done, 2 * g + 2)
                    for i in range(2):
                        for c in range(DT):
                            mm = pe.transpose(tb[g % 2][:, c, i * P:(i + 1) * P], z[(2 * g + i) % 4][:, c * P:(c + 1) * P], T.ident[:])
                    mm.then_inc(turned, 1)
                pe.wait_ge(w_lo, 1)
                pe.wait_ge(z_lo, NT // 2)
                for n, (b, which, g) in enumerate(QK):
                    if n >= 2:
                        pe.wait_ge(qk_lo, n - 1)
                    src = z_t if which == 0 else T.ctx_t
                    cols = slice(g * P, (g + 1) * P)
                    for c in range(DT):
                        mm = three_products(pe, pb[n % 2][:], (w.hi[:, which, c, cols], w.lo[:, which, c, cols]),
                                            (src.hi[:, c, b * S:(b + 1) * S], src.lo[:, c, b * S:(b + 1) * S]), c == 0, c == DT - 1)
                    mm.then_inc(proj, 1)
                for n in range(NV):
                    pe.wait_ge(qk_lo, min(nqk, nqk + n - 1))
                    if n >= 2:
                        pe.wait_ge(v_ready, n - 1)
                    for i in range(2):
                        rows = slice((2 * n + i) * P, (2 * n + i + 1) * P)
                        for c in range(DT):
                            mm = three_products(pe, pb[n % 2][:, i * D:(i + 1) * D], (T.ctx_t.hi[:, c, rows], T.ctx_t.lo[:, c, rows]),
                                                (w.hi[:, 2, c, :], w.lo[:, 2, c, :]), c == 0, c == DT - 1)
                    mm.then_inc(proj, 1)


def phase_attention1(nc, sem, T, dram):
    NBUF = 4
    TURN_LAG, ATTEND_LAG = 3, 5
    with ExitStack() as ctx:
        sb, ps = make_tensors(nc, ctx)
        stack = [[sb(f"d_{n}{i}", [STACK, 2, S], F16) for i in range(2)] for n in "qk"]
        wo_raw, wo = sb("d_wo_raw", [P, DT, D]), Split(sb, "d_wo", [P, DT, D])
        o_t = [Split(sb, f"d_o_t{i}", [P, 2, DT, P]) for i in range(2)]
        o = sb("d_o", [P, QT, D])
        masked = [sb(f"d_masked{i}", [P, 3 * P]) for i in range(NBUF)]
        e = [sb(f"d_e{i}", [P, 3 * P]) for i in range(NBUF)]
        e_t = [Split(sb, f"d_e_t{i}", [P, 3, P]) for i in range(NBUF)]
        neg_max, den, rden = sb("d_neg_max", [P, 2, UNITS]), sb("d_den", [P, 2, UNITS]), sb("d_rden", [P, UNITS])
        sums = sb("d_sums", [P, UNITS, DH])
        gate = sb("d_gate", [1, 2 * UNITS])
        expert_raw = [sb(f"d_expert_raw{k}", [P, MATRIX]) for k in range(3)]
        expert_raw_in = [sem(f"dexpert_raw_in{k}") for k in range(3)]
        expert_hi, expert_lo = sem("dexpert_hi"), sem("dexpert_lo")
        sc = [ps(f"d_sc{i}", [P, 512]) for i in range(NBUF)]
        et = [ps(f"d_et{i}", [P, 4, P]) for i in range(2)]
        ob = [ps(f"d_ob{i}", [P, 512]) for i in range(2)]
        cb = sc[NBUF - 2:]
        names = ("wo_in", "wo_hi", "wo_lo", "loaded0", "loaded1", "scores", "masked_ok", "exp_ok", "turned", "et_hi", "et_lo", "pv_done", "rden_ok",
                 "normed", "close_full", "close_hi", "close_free")
        (wo_in, wo_hi, wo_lo, loaded0, loaded1, scores, masked_ok, exp_ok, turned, et_hi, et_lo, pv_done, rden_ok,
         normed, close_full, close_hi, close_free) = (sem("d" + n) for n in names)
        loaded = (loaded0, loaded1)
        CLOSE = [("T", 0), ("T", 1), ("W", 0), ("W", 1), ("W", 2), ("W", 3)]
        LAST_M = PAIRS // 2 - 1
        BU = PAIRS * UNITS

        def unit(b, m, par, j):
            return b * BU + m * (2 * UNITS) + (par * UNITS + j)

        def lagged(m, par, j, lag):
            n = par * UNITS + j - lag
            return (m, n // UNITS, n % UNITS) if n >= 0 else (m - 1, 1, n + UNITS)

        def run_pairs(eng, unit_step, drain, closing):
            with eng.Fori(0, B) as b:
                def two_pairs(m, first, last):
                    for par in range(2):
                        for j in range(UNITS):
                            unit_step(b, m, par, j, first and par == 0, last and par == 1)

                two_pairs(0, True, False)
                with eng.Fori(1, PAIRS // 2 - 1) as m:
                    two_pairs(m, False, False)
                two_pairs(LAST_M, False, True)
                drain(b)
                closing(b)

        with nc.Block() as block:

            @block.sync
            def _(sp):
                sp.dma_start(wo_raw[:], dram["wo1"].rearrange("(c p) n -> p c n", p=P)).then_inc(wo_in, 16)
                sp.sem_inc(scores, 2 * UNITS)
                with sp.Fori(0, B) as b:
                    with sp.Fori(0, PAIRS // 2) as m:
                        for par in range(2):
                            sp.wait_ge(scores, b * BU + m * (2 * UNITS) + (par + 1) * UNITS)
                            for which in range(2):
                                sp.dma_start(stack[which][par][:], dram["stack"][which, bass.ds(b, 1), :, bass.ds(m * 4 + par * 2, 2), :].rearrange("o c h t -> c (o h) t"))\
                                    .then_inc(loaded[par], 16)

            @block.gpsimd
            def _(pool):
                pool.wait_ge(wo_hi, 1)
                pool.tensor_tensor(wo.lo[:], wo_raw[:], wo.hi[:], ALU.subtract).then_inc(wo_lo, 1)
                split_experts(pool, dram, expert_raw, expert_raw_in, T.experts1, expert_hi, expert_lo)

            @block.scalar
            def _(act):
                act.wait_ge(wo_in, 16)
                nc.scalar.activation(wo.hi[:], wo_raw[:], ACT.Copy).then_inc(wo_hi, 1)

                def turned_part(b, m, par, j):
                    n = window(j % QT)[1]
                    act.wait_ge(turned, unit(b, m, par, j) + (NBUF + 1))
                    act.wait_ge(pv_done, unit(b, m, par, j) + 1)
                    nc.scalar.activation(e_t[j % NBUF].hi[:, 0:n, :], et[j % 2][:, 0:n, :], ACT.Copy).then_inc(et_hi, 1)

                def unit_step(b, m, par, j, first, last):
                    u = unit(b, m, par, j)
                    if not (first and j < TURN_LAG):
                        turned_part(b, *lagged(m, par, j, TURN_LAG))
                    n = window(j % QT)[1] * P
                    act.wait_ge(masked_ok, u + (NBUF + 1))
                    act.wait_ge(turned, u + 1)
                    if j == 0:
                        act.wait_ge(normed, b * PAIRS + m * 2 + (par + 1))
                    nc.scalar.activation(e[j % NBUF][:, 0:n], masked[j % NBUF][:, 0:n], ACT.Exp, bias=neg_max[:, par, j:j + 1], scale=-1.0,
                                         accum_out=den[:, par, j:j + 1]).then_inc(exp_ok, 1)

                def drain(b):
                    for j in range(UNITS - TURN_LAG, UNITS):
                        turned_part(b, LAST_M, 1, j)

                def closing(b):
                    for i, (what, t) in enumerate(CLOSE[:2]):
                        act.wait_ge(close_full, b * len(CLOSE) + (i + 1))
                        nc.scalar.activation(o_t[i].hi[:].rearrange("p a c n -> p (a c n)"), cb[i][:], ACT.Copy).then_inc(close_hi, 1)

                act.sem_inc(exp_ok, NBUF)
                run_pairs(act, unit_step, drain, closing)

            @block.vector
            def _(dve):
                def turned_part(b, m, par, j):
                    n = window(j % QT)[1]
                    dve.wait_ge(et_hi, unit(b, m, par, j) + 1)
                    nc.vector.tensor_tensor(e_t[j % NBUF].lo[:, 0:n, :], et[j % 2][:, 0:n, :], e_t[j % NBUF].hi[:, 0:n, :],
                                            ALU.subtract).then_inc(et_lo, 1)

                def normalize(b, m, par):
                    dve.wait_ge(pv_done, unit(b, m, par, UNITS - 1) + (NBUF + 1))
                    nc.vector.reciprocal(rden[:], den[:, par, :]).then_inc(rden_ok, 1)
                    nc.vector.tensor_reduce(sums[:], ob[par][:, 0:UNITS * 2 * DH].rearrange("p (u w d) -> p u d w", w=2, d=DH), AX.X, ALU.add).then_inc(rden_ok, 1)
                    dve.wait_ge(rden_ok, b * (PAIRS * 2) + m * 4 + (par * 2 + 2))
                    for a in range(2):
                        op = nc.vector.tensor_tensor(o[:, :, bass.ds(m * (4 * DH) + (par * 2 + a) * DH, DH)],
                                                     sums[:, a * QT:(a + 1) * QT, :],
                                                     rden[:, a * QT:(a + 1) * QT].unsqueeze(2).to_broadcast([P, QT, DH]), ALU.mult)
                    op.then_inc(normed, 1)

                def unit_step(b, m, par, j, first, last):
                    u = unit(b, m, par, j)
                    start, n = window(j % QT)
                    off = (start - (j % QT - 1)) * P
                    dve.wait_ge(scores, u + (1 + 2 * UNITS))
                    dve.wait_ge(exp_ok, u + 1)
                    nc.vector.memset(gate[:, par * UNITS + j:par * UNITS + j + 1], 0.0)
                    nc.vector.tensor_tensor_reduce(masked[j % NBUF][:, 0:n * P], sc[j % NBUF][:, 0:n * P], T.band[:, off:off + n * P],
                                                   -SCALE1, 3e38, ALU.add, ALU.min, neg_max[:, par, j:j + 1]).then_inc(masked_ok, 1)
                    if not (first and j < TURN_LAG):
                        turned_part(b, *lagged(m, par, j, TURN_LAG))
                    if j == ATTEND_LAG + 1 and not first:
                        normalize(b, *((m, 0) if par == 1 else (m - 1, 1)))

                def drain(b):
                    for j in range(UNITS - TURN_LAG, UNITS):
                        turned_part(b, LAST_M, 1, j)
                    normalize(b, LAST_M, 1)

                def closing(b):
                    for i, (what, t) in enumerate(CLOSE):
                        g = b * len(CLOSE) + i
                        if what == "T":
                            dve.wait_ge(close_hi, b * 2 + (i + 1))
                            nc.vector.tensor_tensor(o_t[i].lo[:].rearrange("p a c n -> p (a c n)"), cb[i][:],
                                                    o_t[i].hi[:].rearrange("p a c n -> p (a c n)"), ALU.subtract).then_inc(close_free, 1)
                        else:
                            dve.wait_ge(close_full, g + 1)
                            xt = T.x[:, bass.ds(b * QT + t, 1), :].rearrange("p o d -> p (o d)")
                            nc.vector.tensor_tensor(xt, cb[i % 2][:, 0:D], xt, ALU.add).then_inc(close_free, 1)

                dve.sem_inc(masked_ok, NBUF)
                dve.sem_inc(turned, NBUF)
                dve.sem_inc(et_lo, 2)
                dve.sem_inc(normed, 2)
                dve.sem_inc(close_free, 2)
                run_pairs(dve, unit_step, drain, closing)

            @block.tensor
            def _(pe):
                pe.wait_ge(wo_lo, 1)

                def unit_step(b, m, par, j, first, last):
                    a, qt = j // QT, j % QT
                    u = unit(b, m, par, j)
                    start, n = window(qt)
                    if j == 0:
                        pe.wait_ge(loaded[par], b * (PAIRS * 16) + m * 32 + 32)
                    pe.wait_ge(masked_ok, u + 1)
                    if first and j == NBUF - 2:
                        pe.wait_ge(close_free, b * len(CLOSE) + 2)
                    pe.matmul(sc[j % NBUF][:, 0:n * P], stack[0][par][:, a, qt * P:(qt + 1) * P], stack[1][par][:, a, start * P:(start + n) * P],
                              start=True, stop=True).then_inc(scores, 1)
                    if not (first and j < TURN_LAG):
                        turn(b, *lagged(m, par, j, TURN_LAG))
                    if not (first and j < ATTEND_LAG):
                        attend(b, *lagged(m, par, j, ATTEND_LAG))

                def turn(b, m, par, j):
                    pe.wait_ge(exp_ok, unit(b, m, par, j) + (NBUF + 1))
                    pe.wait_ge(et_lo, unit(b, m, par, j) + 1)
                    for kt in range(window(j % QT)[1]):
                        mm = pe.transpose(et[j % 2][:, kt, :], e[j % NBUF][:, kt * P:(kt + 1) * P], T.ident[:])
                    mm.then_inc(turned, 1)

                def attend(b, m, par, j):
                    a, qt = j // QT, j % QT
                    start, n = window(qt)
                    if j == 0:
                        pe.wait_ge(normed, b * PAIRS + m * 2 + (par + 1))
                    pe.wait_ge(et_lo, unit(b, m, par, j) + 3)
                    for kt in range(n):
                        vv = T.v1[:, bass.ds(b * QT + (start + kt), 1), bass.ds(m * 4 + (par * 2 + a), 1), :, :].rearrange("p o h w d -> p (o h w d)")
                        out = ob[par][:, j * 2 * DH:(j + 1) * 2 * DH]
                        pe.matmul(out, e_t[j % NBUF].hi[:, kt, :], vv, start=(kt == 0), stop=False)
                        mm = pe.matmul(out, e_t[j % NBUF].lo[:, kt, :], vv, start=False, stop=(kt == n - 1))
                    mm.then_inc(pv_done, 1)

                def drain(b):
                    for j in range(UNITS, UNITS + ATTEND_LAG):
                        if j < UNITS + TURN_LAG:
                            turn(b, LAST_M, 1, j - TURN_LAG)
                        attend(b, LAST_M, 1, j - ATTEND_LAG)

                def closing(b):
                    for i, (what, t) in enumerate(CLOSE):
                        pe.wait_ge(close_free, b * len(CLOSE) + (i + 1))
                        if what == "T":
                            if i == 0:
                                pe.wait_ge(normed, b * PAIRS + (PAIRS + 2))
                            for n in range(4):
                                a, c = n // DT, n % DT
                                mm = pe.transpose(cb[i][:, n * P:(n + 1) * P], o[:, 2 * t + a, c * P:(c + 1) * P], T.ident[:])
                        else:
                            if t == 0:
                                pe.wait_ge(close_free, b * len(CLOSE) + 4)
                            for c in range(DT):
                                ot = o_t[t // 2]
                                mm = three_products(pe, cb[i % 2][:, 0:D], (ot.hi[:, t % 2, c, :], ot.lo[:, t % 2, c, :]),
                                                    (wo.hi[:, c, :], wo.lo[:, c, :]), c == 0, c == DT - 1)
                        mm.then_inc(close_full, 1)

                pe.sem_inc(pv_done, NBUF)
                run_pairs(pe, unit_step, drain, closing)


GROUPS1 = 4
PER_GROUP = 2
EXPERTS1 = GROUPS1 * PER_GROUP
FF1 = 512
FT1 = FF1 // P
TILE = 2 * P
TILES1 = B * S // TILE + GROUPS1 - 1
ROW = D + PER_GROUP
MATRIX = DT * FF1
GATE1, UP1, DOWN1 = 0, MATRIX, 2 * MATRIX
EXPERT_COLS = 3 * MATRIX


def load_expert(pool, dram, raw, raw_in, e):
    for k, name in enumerate(("gate_w", "up_w", "down_w")):
        n = dram[name].shape[2]
        pool.dma_start(raw[k][:].rearrange("p (c n) -> p c n", n=n), dram[name][e].rearrange("(c p) n -> p c n", p=P)).then_inc(raw_in[k], 16)


def split_experts(pool, dram, raw, raw_in, w, w_hi, w_lo):
    load_expert(pool, dram, raw, raw_in, 0)
    for e in range(EXPERTS1):
        for k in range(3):
            cols = slice(e * EXPERT_COLS + k * MATRIX, e * EXPERT_COLS + (k + 1) * MATRIX)
            pool.wait_ge(raw_in[k], 16 * (e + 1))
            pool.tensor_copy(w.hi[:, cols], raw[k][:]).then_inc(w_hi, 1)
            pool.wait_ge(w_hi, 3 * e + k + 1)
            pool.tensor_tensor(w.lo[:, cols], raw[k][:], w.hi[:, cols], ALU.subtract).then_inc(w_lo, 1)
        if e + 1 < EXPERTS1:
            pool.wait_ge(w_lo, 3 * (e + 1))
            load_expert(pool, dram, raw, raw_in, e + 1)


def phase_route1(nc, sem, T, dram):
    with ExitStack() as ctx:
        sb, ps = make_tensors(nc, ctx)
        stats, mv, sd, rstd = sb("g_stats", [P, NT, 6]), sb("g_mv", [P, NT, 2]), sb("g_sd", [P, NT]), sb("g_rstd", [P, NT])
        rows = sb("g_rows", [P, NT, ROW])
        xf_t = sb("g_xf_t", [P, DT, B * S])
        LOGITS = GROUPS1 + EXPERTS1
        router = sb("g_router", [P, DT, LOGITS])
        sig = sb("g_sig", [P, NT, LOGITS])
        macro = sig[:, :, 0:GROUPS1]
        micro = sig[:, :, GROUPS1:LOGITS].rearrange("p t (g e) -> p t g e", e=PER_GROUP)
        best, best_sum, best_value = sb("g_best", [P, NT]), sb("g_best_sum", [P, NT]), sb("g_best_value", [P, NT])
        order, thresholds, tiles = sb("g_order", [P, GROUPS1]), sb("g_thresholds", [P, B * S // TILE]), sb("g_tiles", [P, TILES1])
        marks, mark = sb("g_marks", [P, NT, GROUPS1]), sb("g_mark", [P, NT])
        chosen = sb("g_chosen", [P, NT, GROUPS1], F16)
        micro_sum, share = sb("g_micro_sum", [P, NT, GROUPS1]), sb("g_share", [P, NT, GROUPS1])
        parts = sb("g_parts", [P, NT, PER_GROUP, GROUPS1])
        ones, tri, zeros = sb("g_ones", [P, P], F16), sb("g_tri", [P, P], F16), sb("g_zeros", [P, NT, GROUPS1], F16)
        full = sb("g_full", [P, GROUPS1, B * S // TILE])
        count, first_tile = sb("g_count", [P, GROUPS1]), sb("g_first_tile", [P, GROUPS1])
        past = sb("g_past", [P, TILES1, GROUPS1 - 1])
        tile_group_f, place, place_sum = sb("g_tile_group_f", [P, TILES1]), sb("g_place", [P, NT, GROUPS1]), sb("g_place_sum", [P, NT])
        blank = sb("g_blank", [P, ROW])
        tb = [ps(f"g_tb{i}", [P, DT, 2 * P]) for i in range(2)]
        lb, cb, rb = (ps(n, [P, 512]) for n in ("g_lb", "g_cb", "g_rb"))
        logit_bank = lb[:, 0:NT * LOGITS].rearrange("p (t e) -> p t e", e=LOGITS)
        rank_bank = rb[:, 0:NT * GROUPS1].rearrange("p (t e) -> p t e", e=GROUPS1)
        names = ("router_in", "xf_done", "turned", "copied", "logits", "sig_ok", "consts",
                 "blanked", "v", "chosen_ok", "counted", "ranked", "rows_ok", "sorted_")
        (router_in, xf_done, turned, copied, logits, sig_ok, consts,
         blanked, v, chosen_ok, counted, ranked, rows_ok, sorted_) = (sem("g" + n) for n in names)
        with nc.Block() as block:

            @block.sync
            def _(sp):
                sp.dma_start(router[:, :, 0:GROUPS1], dram["macro"].rearrange("(c p) g -> p c g", p=P)).then_inc(router_in, 16)
                sp.dma_start(router[:, :, GROUPS1:LOGITS], dram["micro"].rearrange("(c p) e -> p c e", p=P)).then_inc(router_in, 16)
                sp.wait_ge(consts, 1)
                sp.dma_start(dram["sorted"].rearrange("(t p) d -> p t d", p=P),
                             blank[:].unsqueeze(1).to_broadcast([P, TILES1 * TILE // P, ROW])).then_inc(blanked, 16)

            @block.gpsimd
            def _(pool):
                pool.memset(blank[:], 0.0).then_inc(consts, 1)
                pool.memset(zeros[:], 0.0).then_inc(consts, 1)
                pool.memset(ones[:], 1.0).then_inc(consts, 1)
                pool.wait_ge(consts, 3)
                pool.affine_select(out=tri[:], in_=ones[:], compare_op=ALU.is_gt, fill=0.0, base=0,
                                   pattern=[[1, P]], channel_multiplier=-1).then_inc(consts, 1)
                pool.iota(order[:], pattern=[[-1, GROUPS1]], base=GROUPS1, channel_multiplier=0, allow_small_or_imprecise_dtypes=True).then_inc(consts, 1)
                pool.iota(thresholds[:], pattern=[[TILE, B * S // TILE]], base=0, channel_multiplier=0, allow_small_or_imprecise_dtypes=True).then_inc(consts, 1)
                pool.iota(tiles[:], pattern=[[1, TILES1]], base=0, channel_multiplier=0, allow_small_or_imprecise_dtypes=True).then_inc(consts, 1)
                pool.wait_ge(blanked, 16)
                pool.wait_ge(rows_ok, 2)
                for t in range(NT):
                    pool.indirect_dma_start(out=dram["sorted"], out_offset=bass.IndirectOffsetOnAxis(ap=T.place[:, t:t + 1], axis=0),
                                            in_=rows[:, t, :], in_offset=None).then_inc(sorted_, 16)
                pool.wait_ge(sorted_, 16 * NT)

            @block.scalar
            def _(act):
                layernorm_root(nc, act, T, 4, sd)
                for g in range(NT // 2):
                    act.wait_ge(turned, g + 1)
                    nc.scalar.activation(xf_t[:, :, g * 2 * P:(g + 1) * 2 * P], tb[g % 2][:], ACT.Copy).then_inc(copied, 1)
                act.wait_ge(logits, 1)
                nc.scalar.activation(sig[:], logit_bank, ACT.Sigmoid).then_inc(sig_ok, 1)

            @block.tensor
            def _(pe):
                for g in range(NT // 2):
                    if g >= 2:
                        pe.wait_ge(copied, g - 1)
                    pe.wait_ge(xf_done, 2 * g + 2)
                    for i in range(2):
                        for c in range(DT):
                            mm = pe.transpose(tb[g % 2][:, c, i * P:(i + 1) * P], rows[:, 2 * g + i, c * P:(c + 1) * P], T.ident[:])
                    mm.then_inc(turned, 1)
                pe.wait_ge(router_in, 32)
                pe.wait_ge(copied, NT // 2)
                for t in range(NT):
                    for c in range(DT):
                        mm = pe.matmul(logit_bank[:, t, :], xf_t[:, c, t * P:(t + 1) * P], router[:, c, :], start=(c == 0), stop=(c == DT - 1))
                mm.then_inc(logits, 1)
                pe.wait_ge(consts, 4)
                pe.wait_ge(chosen_ok, 1)
                for t in range(NT):
                    mm = pe.matmul(cb[:, 0:GROUPS1], ones[:], chosen[:, t, :], start=(t == 0), stop=(t == NT - 1))
                mm.then_inc(counted, 1)
                prefix_counts(pe, rank_bank, chosen, tri, ones, zeros, GROUPS1).then_inc(ranked, 1)

            @block.vector
            def _(dve):
                steps = [0]

                def step_done(op):
                    steps[0] += 1
                    op.then_inc(v, 1)
                    dve.wait_ge(v, steps[0])

                def ahead(op):
                    steps[0] += 1
                    op.then_inc(v, 1)

                def over_groups(a):
                    return a[:].unsqueeze(2).to_broadcast([P, NT, GROUPS1])

                layernorm_stats(nc, dve, T, 4, T.x, stats, mv, sd)
                step_done(nc.vector.reciprocal(rstd[:], sd[:]))
                for t in range(NT):
                    nc.vector.tensor_scalar(rows[:, t, 0:D], T.x[:, t, :], mv[:, t, 0:1], rstd[:, t:t + 1], ALU.subtract, ALU.mult).then_inc(xf_done, 1)
                dve.wait_ge(consts, 7)
                dve.wait_ge(sig_ok, 1)
                step_done(nc.vector.tensor_reduce(best[:], macro, AX.X, ALU.max))
                step_done(nc.vector.tensor_tensor(marks[:], macro, over_groups(best), ALU.is_equal))
                step_done(nc.vector.tensor_tensor(marks[:], marks[:], order[:].unsqueeze(1).to_broadcast([P, NT, GROUPS1]), ALU.mult))
                step_done(nc.vector.tensor_reduce(mark[:], marks[:], AX.X, ALU.max))
                nc.vector.tensor_tensor(chosen[:], marks[:], over_groups(mark), ALU.is_equal).then_inc(chosen_ok, 1)
                ahead(nc.vector.tensor_scalar(best_sum[:], best[:], 1e-9, None, ALU.add))
                step_done(nc.vector.tensor_tensor(micro_sum[:], micro[:, :, :, 0], micro[:, :, :, 1], ALU.add))
                ahead(nc.vector.reciprocal(best_value[:], best_sum[:]))
                step_done(nc.vector.tensor_scalar(micro_sum[:], micro_sum[:], 1e-9, None, ALU.add))
                ahead(nc.vector.tensor_tensor(best_value[:], best_value[:], best[:], ALU.mult))
                step_done(nc.vector.reciprocal(share[:], micro_sum[:]))
                dve.wait_ge(chosen_ok, 1)
                step_done(nc.vector.tensor_tensor(share[:], share[:], chosen[:], ALU.mult))
                step_done(nc.vector.tensor_tensor(share[:], share[:], over_groups(best_value), ALU.mult))
                step_done(nc.vector.tensor_tensor(parts[:], micro.rearrange("p t g e -> p t e g"),
                                                  share[:].unsqueeze(2).to_broadcast([P, NT, PER_GROUP, GROUPS1]), ALU.mult))
                nc.vector.tensor_reduce(rows[:, :, D:ROW], parts[:], AX.X, ALU.add).then_inc(rows_ok, 1)
                dve.wait_ge(counted, 1)
                step_done(nc.vector.tensor_tensor(full[:], cb[:, 0:GROUPS1].unsqueeze(2).to_broadcast([P, GROUPS1, B * S // TILE]),
                                                  thresholds[:].unsqueeze(1).to_broadcast([P, GROUPS1, B * S // TILE]), ALU.is_gt))
                ahead(nc.vector.memset(first_tile[:, 0:1], 0.0))
                step_done(nc.vector.tensor_reduce(count[:], full[:], AX.X, ALU.add))
                for g in range(1, GROUPS1):
                    step_done(nc.vector.tensor_tensor(first_tile[:, g:g + 1], first_tile[:, g - 1:g], count[:, g - 1:g], ALU.add))
                dve.wait_ge(ranked, 1)
                ahead(nc.vector.scalar_tensor_tensor(out=place[:], in0=first_tile[:].unsqueeze(1).to_broadcast([P, NT, GROUPS1]), scalar=float(TILE),
                                                     in1=rank_bank, op0=ALU.mult, op1=ALU.add))
                step_done(nc.vector.tensor_tensor(past[:], tiles[:].unsqueeze(2).to_broadcast([P, TILES1, GROUPS1 - 1]),
                                                  first_tile[:, 1:GROUPS1].unsqueeze(1).to_broadcast([P, TILES1, GROUPS1 - 1]), ALU.is_ge))
                step_done(nc.vector.tensor_tensor(place[:], place[:], chosen[:], ALU.mult))
                ahead(nc.vector.tensor_reduce(place_sum[:], place[:], AX.X, ALU.add))
                step_done(nc.vector.tensor_reduce(tile_group_f[:], past[:], AX.X, ALU.add))
                nc.vector.tensor_copy(T.place[:], place_sum[:]).then_inc(rows_ok, 1)
                nc.vector.tensor_copy(T.tile_group[:], tile_group_f[:])


def phase_experts1(nc, sem, T, dram):
    with ExitStack() as ctx:
        sb, ps = make_tensors(nc, ctx)
        rows = [sb(f"h_rows{i}", [P, 2, ROW]) for i in range(2)]
        weight = [sb(f"h_weight{i}", [P, 2, PER_GROUP]) for i in range(2)]
        xt = [Split(sb, f"h_xt{i}", [P, DT, TILE]) for i in range(2)]
        silu = [sb(f"h_silu{i}", [P, TILE]) for i in range(2)]
        h = [sb(f"h_h{i}", [P, TILE]) for i in range(2)]
        HT = PER_GROUP * FT1
        hs = [Split(sb, f"h_hs{i}", [P, HT, TILE]) for i in range(2)]
        first = [sb(f"h_first{i}", [P, 2, D]) for i in range(2)]
        res = [sb(f"h_res{i}", [P, 2, D]) for i in range(2)]
        tb = [ps(f"h_tb{i}", [P, DT, TILE]) for i in range(2)]
        hb = [ps(f"h_hb{i}", [P, 2, TILE]) for i in range(2)]
        ob = [[ps(f"h_ob{i}_{n}", [P, PER_GROUP, D]) for n in range(2)] for i in range(2)]
        names = ("rows_in0", "rows_in1", "turned", "xt_hi", "rows_free", "xt_lo", "h_full", "silu_ok", "h_ok", "h_hi", "h_lo", "out_done",
                 "first_ok", "res_ok", "res_free", "stored")
        (rows_in0, rows_in1, turned, xt_hi, rows_free, xt_lo, h_full, silu_ok, h_ok, h_hi, h_lo, out_done,
         first_ok, res_ok, res_free, stored) = (sem("h" + n) for n in names)
        rows_in = (rows_in0, rows_in1)

        def run_tiles(eng, head, tail):
            head(0, 0)
            with eng.Fori(0, TILES1 // 2) as m:
                head(m * 2 + 1, 1)
                tail(m * 2, 0)
                head(m * 2 + 2, 0)
                tail(m * 2 + 1, 1)
            tail(TILES1 - 1, 0)

        with nc.Block() as block:

            @block.sync
            def _(sp):
                def load(j):
                    sp.dma_start(rows[j % 2][:], dram["sorted"][j * TILE:(j + 1) * TILE, :].rearrange("(n p) d -> p n d", p=P)).then_inc(rows_in[j % 2], 16)

                load(0)
                load(1)
                sp.sem_inc(res_free, 2)
                for j in range(TILES1):
                    if j + 2 < TILES1:
                        sp.wait_ge(rows_free, j + 1)
                        load(j + 2)
                    sp.wait_ge(res_ok, j + 3)
                    if j >= 1:
                        sp.wait_ge(stored, 16 * j)
                        sp.sem_inc(res_free, 1)
                    sp.dma_start(dram["mixed"][j * TILE:(j + 1) * TILE, :].rearrange("(n p) d -> p n d", p=P), res[j % 2][:]).then_inc(stored, 16)
                sp.wait_ge(stored, 16 * TILES1)

            @block.scalar
            def _(act):
                def head(j, i):
                    act.wait_ge(turned, j + 1)
                    nc.scalar.activation(xt[i].hi[:], tb[i][:], ACT.Copy).then_inc(xt_hi, 1)
                    for g in range(HT + 1):
                        if g < HT:
                            act.wait_ge(h_full, j * HT + (g + 1))
                            act.wait_ge(h_ok, j * HT + (g + 1))
                            nc.scalar.activation(silu[g % 2][:], hb[g % 2][:, 0, :], ACT.Silu).then_inc(silu_ok, 1)
                        if g >= 1:
                            act.wait_ge(h_ok, j * HT + (g + 2))
                            if g == 1:
                                act.wait_ge(out_done, j + 1)
                            nc.scalar.activation(hs[i].hi[:, g - 1, :], h[(g - 1) % 2][:], ACT.Copy).then_inc(h_hi, 1)

                run_tiles(act, head, lambda j, i: None)

            @block.vector
            def _(dve):
                def head(j, i):
                    dve.wait_ge(xt_hi, j + 1)
                    dve.wait_ge(res_ok, j + 1)
                    nc.vector.tensor_copy(weight[i][:], rows[i][:, :, D:ROW]).then_inc(rows_free, 1)
                    nc.vector.tensor_tensor(xt[i].lo[:], tb[i][:], xt[i].hi[:], ALU.subtract).then_inc(xt_lo, 1)
                    for g in range(HT + 1):
                        if g < HT:
                            dve.wait_ge(silu_ok, j * HT + (g + 1))
                            dve.wait_ge(h_lo, j * HT + (g + 1))
                            nc.vector.tensor_tensor(h[g % 2][:], hb[g % 2][:, 1, :], silu[g % 2][:], ALU.mult).then_inc(h_ok, 1)
                        if g >= 1:
                            dve.wait_ge(h_hi, j * HT + g)
                            nc.vector.tensor_tensor(hs[i].lo[:, g - 1, :], h[(g - 1) % 2][:], hs[i].hi[:, g - 1, :], ALU.subtract).then_inc(h_lo, 1)

                def tail(j, i):
                    dve.wait_ge(out_done, j + 3)
                    dve.wait_ge(res_ok, j + 1)
                    for n in range(2):
                        nc.vector.tensor_scalar(first[i][:, n, :], ob[i][n][:, 0, :], weight[i][:, n, 0:1], None, ALU.mult).then_inc(first_ok, 1)
                    dve.wait_ge(first_ok, j * 2 + 2)
                    dve.wait_ge(res_free, j + 1)
                    for n in range(2):
                        op = nc.vector.scalar_tensor_tensor(out=res[i][:, n, :], in0=ob[i][n][:, 1, :], scalar=weight[i][:, n, 1:2],
                                                            in1=first[i][:, n, :], op0=ALU.mult, op1=ALU.add)
                    op.then_inc(res_ok, 1)

                dve.sem_inc(xt_lo, 2)
                dve.sem_inc(h_ok, 2)
                dve.sem_inc(h_lo, 2)
                dve.sem_inc(res_ok, 2)
                run_tiles(dve, head, tail)

            @block.tensor
            def _(pe):
                def expert_base(j):
                    group = pe.value_load(T.tile_group[0:1, bass.ds(j, 1)], min_val=0, max_val=GROUPS1 - 1)
                    return group * (PER_GROUP * EXPERT_COLS)

                def weights(base, col, n):
                    cols = bass.ds(base + col, n)
                    return T.experts1.hi[:, cols], T.experts1.lo[:, cols]

                def head(j, i):
                    base = expert_base(j)
                    pe.wait_ge(xt_lo, j + 1)
                    pe.wait_ge(rows_in[i], (j - i) * 8 + 16)
                    for n in range(2):
                        for c in range(DT):
                            mm = pe.transpose(tb[i][:, c, n * P:(n + 1) * P], rows[i][:, n, c * P:(c + 1) * P], T.ident[:])
                    mm.then_inc(turned, 1)
                    pe.wait_ge(xt_lo, j + 3)
                    for g in range(HT):
                        expert, f = g // FT1, g % FT1
                        pe.wait_ge(h_ok, j * HT + (g + 1))
                        for which, start in enumerate((GATE1, UP1)):
                            for c in range(DT):
                                mm = three_products(pe, hb[g % 2][:, which, :], weights(base, expert * EXPERT_COLS + start + c * FF1 + f * P, P),
                                                    (xt[i].hi[:, c, :], xt[i].lo[:, c, :]), c == 0, c == DT - 1)
                        mm.then_inc(h_full, 1)

                def tail(j, i):
                    base = expert_base(j)
                    pe.wait_ge(h_lo, j * HT + (HT + 2))
                    pe.wait_ge(res_ok, j + 1)
                    for n in range(2):
                        for expert in range(PER_GROUP):
                            for f in range(FT1):
                                g = expert * FT1 + f
                                mm = three_products(pe, ob[i][n][:, expert, :], (hs[i].hi[:, g, n * P:(n + 1) * P], hs[i].lo[:, g, n * P:(n + 1) * P]),
                                                    weights(base, expert * EXPERT_COLS + DOWN1 + f * D, D), f == 0, f == FT1 - 1)
                    mm.then_inc(out_done, 1)

                pe.sem_inc(out_done, 2)
                run_tiles(pe, head, tail)


def phase_output(nc, sem, T, dram, out):
    with ExitStack() as ctx:
        sb, _ = make_tensors(nc, ctx)
        mixed = sb("o_mixed", [P, NT, D])
        gathered = [sem(f"ogathered{n}") for n in range(B)]
        added, stored = sem("oadded"), sem("ostored")
        with nc.Block() as block:

            @block.gpsimd
            def _(pool):
                for t in range(NT):
                    pool.indirect_dma_start(out=mixed[:, t, :], out_offset=None, in_=dram["mixed"],
                                            in_offset=bass.IndirectOffsetOnAxis(ap=T.place[:, t:t + 1], axis=0)).then_inc(gathered[t // QT], 16)

            @block.vector
            def _(dve):
                for n in range(B):
                    dve.wait_ge(gathered[n], 16 * QT)
                    part = slice(n * QT, (n + 1) * QT)
                    nc.vector.tensor_tensor(T.x[:, part, :], T.x[:, part, :], mixed[:, part, :], ALU.add).then_inc(added, 1)

            @block.sync
            def _(sp):
                for n in range(B):
                    sp.wait_ge(added, n + 1)
                    sp.dma_start(out[n * S:(n + 1) * S, :].rearrange("(t p) d -> p t d", p=P), T.x[:, n * QT:(n + 1) * QT, :]).then_inc(stored, 16)
                sp.wait_ge(stored, 16 * B)


class Tensors:
    pass


def build(nc, dram, out):
    sems = ExitStack()

    def sem(name):
        return sems.enter_context(nc.semaphore(name))

    with sems, ExitStack() as keep:
        sb, _ = make_tensors(nc, keep)
        T = Tensors()
        T.stat_done, T.mv_done, T.var_eps, T.sd_done = sem("stat_done"), sem("mv_done"), sem("var_eps"), sem("sd_done")
        T.x = sb("x", [P, NT, D])
        T.ident = sb("ident", [P, P])
        T.ctx_t = Split(sb, "ctx_t", [P, DT, B * S])
        T.slot_token = sb("slot_token", [P, EXPERTS0, HALVES], I32)
        T.slot_weight = sb("slot_weight", [P, EXPERTS0, HALVES])
        with ExitStack() as part:
            sb0, _ = make_tensors(nc, part)
            T.z_t = Split(sb0, "z_t", [P, DT, B * S])
            T.wq0 = Split(sb0, "wq0", [P, DT, CW])
            T.wk0 = Split(sb0, "wk0", [P, DT, CW])
            T.wv0 = Split(sb0, "wv0", [P, DT, CW])
            T.wo0 = Split(sb0, "wo0", [P, CT, D])
            phase_prepare(nc, sem, sb, T, dram)
            phase_attention0(nc, sem, T, dram)
        phase_route0(nc, sem, T, dram)
        phase_experts0(nc, sem, T, dram)
        T.place = sb("place", [P, NT], I32)
        T.tile_group = sb("tile_group", [P, TILES1], I32)
        T.experts1 = Split(sb, "experts1", [P, EXPERTS1 * EXPERT_COLS])
        with ExitStack() as part:
            sb1, _ = make_tensors(nc, part)
            T.v1 = sb1("v1", [P, NT, HEADS, 2, DH], F16)
            T.band = sb1("band", [P, 3 * P], BF16)
            phase_project1(nc, sem, T, dram)
            phase_attention1(nc, sem, T, dram)
        phase_route1(nc, sem, T, dram)
        phase_experts1(nc, sem, T, dram)
        phase_output(nc, sem, T, dram, out)


def kernel(**inputs):
    import numpy as _np
    import concourse.bacc as _bacc
    from concourse import mybir as _mybir
    from concourse.bass_utils import run_bass_kernel_spmd as _run

    nc = _bacc.Bacc("TRN2", target_bir_lowering=False, num_devices=1)
    A = {k: _np.asarray(v) for k, v in inputs.items()}

    def columns(a):
        return _np.moveaxis(a.reshape(a.shape[:-1] + (-1, P)), -1, 0)

    host = {
        "x": A["x"].reshape(B * S, D),
        "ctx_t": A["ctx_1024"].reshape(B * S, D).T,
        "mask": A["mask_Bx1xSxS2_ik1"].reshape(B, S, S),
        "gate0": A["L0_ffn_gate_w"].T, "gamma": columns(A["L0_ffn_ln_gamma"]), "beta": columns(A["L0_ffn_ln_beta"]),
        "fc1": A["L0_ffn_fc1s"].transpose(0, 2, 1), "b1": columns(A["L0_ffn_b1s"]), "fc2": A["L0_ffn_fc2s"].transpose(0, 2, 1), "b2": A["L0_ffn_b2s"],
        "wq1": A["L1_xattn_Wq"].T, "wk1": A["L1_xattn_Wk"].T, "wv1": A["L1_xattn_Wv"].T, "wo1": A["L1_xattn_Wo"].T,
        "bq1": columns(A["L1_xattn_bq"]), "bk1": columns(A["L1_xattn_bk"]), "bv1": A["L1_xattn_bv"], "bo1": A["L1_xattn_bo"],
        "macro": A["L1_ffn_macro_w"], "micro": A["L1_ffn_micro_w"].transpose(1, 0, 2).reshape(D, EXPERTS1),
        "gate_w": A["L1_ffn_gate_w"], "up_w": A["L1_ffn_up_w"], "down_w": A["L1_ffn_down_w"],
        "wq0": A["L0_xattn_Wq"], "wk0": A["L0_xattn_Wk"], "wv0": A["L0_xattn_Wv"], "wo0": A["L0_xattn_Wo"],
    }
    arrays, dram = {}, {}
    for name, a in host.items():
        a = _np.ascontiguousarray(a)
        arrays[f"in_{name}"] = a
        dram[name] = nc.dram_tensor(f"in_{name}", a.shape, _mybir.dt.from_np(a.dtype), kind="ExternalInput").ap()
    for name in ("acc", "y"):
        dram[name] = nc.dram_tensor(f"scratch_{name}", (B * S, D), F32, kind="Internal").ap()
    dram["sorted"] = nc.dram_tensor("scratch_sorted", (TILES1 * TILE, ROW), F32, kind="Internal").ap()
    dram["mixed"] = nc.dram_tensor("scratch_mixed", (TILES1 * TILE, D), F32, kind="Internal").ap()
    dram["stack"] = nc.dram_tensor("scratch_stack", (2, B, STACK, HEADS, S), F16, kind="Internal").ap()
    out = nc.dram_tensor("out_0", (B * S, D), F32, kind="ExternalOutput").ap()
    build(nc, dram, out)
    r = _run(nc, [arrays], core_ids=[0])
    return r.results[0]["out_0"].reshape(B, S, D)
```
